# Optimizing a Trainium2 kernel written in Bass

```python
import numpy as np
import jax
import jax.numpy as jnp

def _softmax(x, axis=-1):
    return jax.nn.softmax(x, axis=axis)

def _gelu(x):
    return jax.nn.gelu(x, approximate=True)

def _silu(x):
    return jax.nn.silu(x)

def _sigmoid(x):
    return jax.nn.sigmoid(x)

def _layernorm(x, axis=-1, eps=1e-05):
    m = jnp.mean(x, axis=axis, keepdims=True)
    v = jnp.var(x, axis=axis, keepdims=True)
    return (x - m) / jnp.sqrt(v + eps)

def _scatter_add(tgt, idx, src, axis=0):
    return tgt.at[idx].add(src)

def _segment_sum(src, seg, n):
    return jax.ops.segment_sum(src, seg, n)
kernel_name = 'mk_cond_resid_d2_seqx_r2_a6ed5a'

def setup_inputs(seed: int=0):
    np.random.seed(seed)
    _w = jnp.asarray

    def _rec_inputs():
        import jax
        import jax.numpy as jnp
        _rk = jax.random.key(seed)
        x = -0.0003929 + 0.9999 * jax.random.normal(jax.random.fold_in(_rk, 1), (2, 2048, 512), jnp.float32)
        _lenS = 2048 - jax.random.randint(jax.random.fold_in(_rk, 7), (2,), 0, max(1, 2048 // 4) + 1, jnp.int32)
        _lenS2 = 2048 - jax.random.randint(jax.random.fold_in(_rk, 8), (2,), 0, max(1, 2048 // 4) + 1, jnp.int32)
        cond_1024 = jax.random.uniform(jax.random.fold_in(_rk, 11), (2, 512), jnp.float32, 0.0, 0.999994)
        _validS = jnp.arange(2048)[None, :] < _lenS[:, None]
        _validS2 = jnp.arange(2048)[None, :] < _lenS2[:, None]
        _causal = jnp.tril(jnp.ones((2048, 2048), dtype=bool))
        mask_SxS_bk0 = jnp.logical_not(jnp.broadcast_to(_validS[0:1, :], (2048, 2048)))
        return (x, cond_1024, mask_SxS_bk0)
    x, cond_1024, mask_SxS_bk0 = _rec_inputs()

    def _L0_cond_setup():
        import jax, jax.numpy as jnp
        import numpy as np
        DT = 0.001
        T_SUBSTEPS = 4
        key = jax.random.key(seed)
        k1, k2 = jax.random.split(key)
        inputs = jax.random.normal(k1, (32, 256, 512), dtype=jnp.float32)
        initial_state = jax.random.uniform(k2, (32, 512), dtype=jnp.float32)
        return {'inputs': inputs, 'initial_state': initial_state}
    _L0_cond_all = _L0_cond_setup()
    _L0_cond_in = {k: v for k, v in _L0_cond_all.items() if k in ()}
    del _L0_cond_all

    def _L1_cond_setup():
        import jax, jax.numpy as jnp
        import numpy as np
        B, T, D, H = (2, 1024, 512, 16)
        E = D // H
        key = jax.random.key(seed)
        ks = jax.random.split(key, 7)
        s = 1.0 / np.sqrt(D)
        return {'x': jax.random.normal(ks[0], (B, T, D), dtype=jnp.float32), 't': jax.random.normal(ks[1], (B, D), dtype=jnp.float32), 'mask': jnp.tril(jnp.ones((T, T), dtype=bool)), 'Wq': jax.random.normal(ks[2], (D, D), dtype=jnp.float32) * s, 'Wk': jax.random.normal(ks[3], (D, D), dtype=jnp.float32) * s, 'Wv': jax.random.normal(ks[4], (D, D), dtype=jnp.float32) * s, 'Wt': jax.random.normal(ks[5], (D, D), dtype=jnp.float32) * s, 'Wo': jax.random.normal(ks[6], (D, D), dtype=jnp.float32) * s}
    _L1_cond_all = _L1_cond_setup()
    _L1_cond_in = {k: v for k, v in _L1_cond_all.items() if k in ('Wq', 'Wk', 'Wv', 'Wt', 'Wo')}
    del _L1_cond_all
    return {'x': x, 'cond_1024': cond_1024, 'mask_SxS_bk0': mask_SxS_bk0, 'L1_cond_Wq': _L1_cond_in['Wq'], 'L1_cond_Wk': _L1_cond_in['Wk'], 'L1_cond_Wv': _L1_cond_in['Wv'], 'L1_cond_Wt': _L1_cond_in['Wt'], 'L1_cond_Wo': _L1_cond_in['Wo']}

def reference(x, cond_1024, mask_SxS_bk0, L1_cond_Wq, L1_cond_Wk, L1_cond_Wv, L1_cond_Wt, L1_cond_Wo):
    import jax
    import jax.numpy as jnp

    def _L0_cond_ref(inputs, initial_state):
        import jax, jax.numpy as jnp
        import numpy as np
        DT = 0.001
        T_SUBSTEPS = 4
        rates = jax.nn.relu(inputs) * DT

        def step(voltage, rate_t):
            spikes = voltage
            for _ in range(T_SUBSTEPS):
                voltage = voltage + rate_t
                spikes = jnp.floor(voltage)
                voltage = voltage - spikes
            return (voltage, spikes)
        _, all_spikes = jax.lax.scan(step, initial_state, jnp.swapaxes(rates, 0, 1))
        return jnp.swapaxes(all_spikes, 0, 1) / DT

    def _L1_cond_ref(x, t, mask, Wq, Wk, Wv, Wt, Wo):
        import jax, jax.numpy as jnp
        import numpy as np
        B, T, D, H = (2, 1024, 512, 16)
        E = D // H
        b, seq, d = x.shape
        h, e = (H, d // H)
        q = (x @ Wq.T).reshape(b, seq, h, e).transpose(0, 2, 1, 3)
        k = (x @ Wk.T).reshape(b, seq, h, e).transpose(0, 2, 1, 3)
        v = (x @ Wv.T).reshape(b, seq, h, e).transpose(0, 2, 1, 3)
        tp = (t @ Wt.T).reshape(b, h, e)
        a = jnp.einsum('bhe,bhse->bhs', tp, q)
        qmod = jnp.einsum('bhs,bhse->bhe', a, q)
        qmod = jnp.broadcast_to(qmod[:, :, None, :], (b, h, seq, e))
        scores = jnp.einsum('bhte,bhse->bhts', qmod, k) / jnp.sqrt(jnp.asarray(e, x.dtype))
        neg = jnp.asarray(jnp.finfo(scores.dtype).min, scores.dtype)
        scores = jnp.where(mask, scores, neg)
        attn = jax.nn.softmax(scores, axis=-1)
        o = jnp.einsum('bhts,bhse->bhte', attn, v)
        o = o.transpose(0, 2, 1, 3).reshape(b, seq, d)
        return o @ Wo.T
    x = x + _L0_cond_ref(x, cond_1024)
    x = x + _L1_cond_ref(x, cond_1024, mask_SxS_bk0, L1_cond_Wq, L1_cond_Wk, L1_cond_Wv, L1_cond_Wt, L1_cond_Wo)
    return x

_drawn_inputs = setup_inputs


def setup_inputs(seed=0):
    import zlib

    import numpy as np

    out = dict(_drawn_inputs(seed))
    spreads = {}
    factors = {}
    for name, (base, spread) in spreads.items():
        noise = np.random.default_rng([zlib.crc32(name.encode()), seed]).standard_normal(out[name].shape)
        drawn = base * np.exp(spread * noise) if base else spread * noise
        out[name] = jnp.asarray(drawn.astype(out[name].dtype))
    for name, factor in factors.items():
        out[name] = (out[name] * factor).astype(out[name].dtype)
    return out
```

```python
import concourse.bass as bass
from concourse import mybir
from contextlib import ExitStack


def spiking_residual_attention(nc, x, cond, mask, wq, wk, wv, wt, wo, out, FORCE=None):
    fp32 = mybir.dt.float32
    i32 = mybir.dt.int32
    u8 = mybir.dt.uint8
    ALU = mybir.AluOpType
    ACT = mybir.ActivationFunctionType
    AX = mybir.AxisListType.X

    B, SEQ, D = x.shape
    H = 16
    E = D // H
    P = 128
    G = D // P
    SUB = 4
    CHUNK = 512
    NC = SEQ // CHUNK
    TPC = CHUNK // P
    NT = SEQ // P
    HG = P // E
    SLOTS = NC + 1
    DT = 0.001
    PER_SPIKE = 999.99993896484375
    SCALE = float(E) ** -0.5
    NEG = -3.4028234663852886e38
    ARENA = 14400
    TWO23 = 8388608.0

    x_t = x.rearrange("b (t p) d -> b p t d", p=P)
    out_t = out.rearrange("b (t p) d -> b p t d", p=P)
    mask_words = mask.rearrange("(p r) s -> p (r s)", p=P).bitcast(i32)
    row0_words = mask[0:1, :].bitcast(i32)

    def w_rows(w):
        return w.rearrange("(j p) d -> p j d", p=P)

    ctx = ExitStack()
    with ctx:
        def sb(name, shape, dt=fp32):
            return ctx.enter_context(nc.sbuf_tensor(name, shape, dt))

        def pb(name):
            return ctx.enter_context(nc.psum_tensor(name, [P, 512], fp32))

        def sem(name):
            return ctx.enter_context(nc.semaphore(name))

        xn = sb("xn", [P, B * NT, D])
        xT = sb("xT", [P, SLOTS, G, CHUNK])
        wq_sb = sb("wq_sb", [P, G, D])
        wk_sb = sb("wk_sb", [P, G, D])
        wqT = sb("wqT", [P, G, D])
        wvT = sb("wvT", [P, G, D])
        woT = sb("woT", [P, G, D])
        ident = sb("ident", [P, P])
        ones = sb("ones", [P, P])
        headmask = sb("headmask", [P, HG])
        U = sb("U", [P, G, B, H])
        cond_rows = sb("cond_rows", [B * G, P])
        tcol = sb("tcol", [P, G, B])
        tpd = sb("tpd", [P, G, B, HG])
        A_sb = sb("A_sb", [P, 2, TPC * H])
        y_sb = sb("y_sb", [P, G, H])
        qsel = sb("qsel", [P, G, HG])
        w_sb = sb("w_sb", [P, G, H])
        pT = sb("pT", [P, NT * H])
        mx = sb("mx", [P, 1])
        nmx = sb("nmx", [P, 1])
        rinv = sb("rinv", [P, H])
        z_sb = sb("z_sb", [P, G, H])
        osel = sb("osel", [P, G, HG])
        ocol = sb("ocol", [P, G])
        vinit = sb("vinit", [P, B, G])
        rstar = sb("rstar", [P, B * NC, G])
        vend = sb("vend", [P, B * NC, G])
        cnt = sb("cnt", [P, 2])
        vprev = sb("vprev", [P, 2])
        vpre = sb("vpre", [P, 2])
        nvlt = sb("nvlt", [P, 2])
        vstar = sb("vstar", [P, 2])
        spk = sb("spk", [P, 2])
        good = sb("good", [P, 3])
        goodall = sb("goodall", [P, 1])
        xorsum = sb("xorsum", [P, 1])
        verdict = sb("verdict", [P, 1], i32)
        arena = sb("arena", [P, ARENA])
        at = [0]

        def cut(n, fresh=False):
            if fresh:
                at[0] = 0
            at[0] += n
            assert at[0] <= ARENA
            return arena[:, at[0] - n:at[0]]

        rate2 = cut(G * 2 * CHUNK, True).rearrange("p (g n) -> p g n", g=G)
        PATH = 2 * CHUNK + 2
        path = cut(G * PATH).rearrange("p (g n) -> p g n", g=G)
        late = cut(2 * 2 * CHUNK).rearrange("p (g n) -> p g n", g=2)
        steps = cut(CHUNK + 1)
        junk = cut(CHUNK + 1)
        prob_all = cut(SEQ)
        prob = prob_all[0:H, :]
        row0 = prob_all[:, 0:SEQ // 4].bitcast(i32)
        orow = cut(D)
        steps_ii = late[:, 0, 0:CHUNK + 1].bitcast(i32)
        mask0 = cut(SEQ // 4)[0:H, :].bitcast(u8)
        wstage = xT[:, SLOTS - 1, :, :]
        wtT = xT[:, SLOTS - 2, :, :]
        masks = xn[:, NT:2 * NT, :].rearrange("p t d -> p (t d)").bitcast(i32)
        masks_f = xn[:, NT:2 * NT, :].rearrange("p t d -> p (t d)")

        pin = [pb("pin0"), pb("pin1")]
        pbk = [pb("pbk0"), pb("pbk1")]
        pAP = pb("pAP")
        pY = pb("pY")
        pS = pb("pS")
        pM = pb("pM")
        ps_tp = pM[:, 0:8].rearrange("p (j b) -> p j b", b=B)
        ps_U = pM[:, 8:136].rearrange("p (k b h) -> p k b h", k=G, b=B)
        ps_q = pM[:, 136:152].rearrange("p (j h) -> p j h", j=G)
        ps_w = pM[:, 152:216].rearrange("p (k h) -> p k h", k=G)
        ps_sum = pM[:, 216:232]
        ps_z = pM[:, 232:296].rearrange("p (k h) -> p k h", k=G)
        ps_o = pM[:, 296:312].rearrange("p (j h) -> p j h", j=G)

        def chunk_slot(b, c):
            return (b * NC + c) % SLOTS

        USE_WT, USE_WQ, USE_WV, USE_WO = 0, G, 2 * G, 3 * G + TPC

        def use_back(k):
            return 3 * G if k == 0 else 4 * G + k * TPC

        def hm_b():
            return headmask[:, :].unsqueeze(1).to_broadcast([P, G, HG])

        def pe_transpose_tile(dst, src):
            for i, s in enumerate(src):
                last = nc.tensor.transpose(dst[:, i * P:(i + 1) * P], s, ident[:, :])
            return last

        def pe_A(b, c, slot):
            for t in range(TPC):
                for g in range(G):
                    last = nc.tensor.matmul(pAP[:, t * H:(t + 1) * H], xT[:, slot, g, t * P:(t + 1) * P],
                                            U[:, g, b, :], start=(g == 0), stop=(g == G - 1))
            return last

        def pe_Y(b, c, par):
            for t in range(TPC):
                for k in range(G):
                    first = c == 0 and t == 0
                    last = nc.tensor.matmul(pY[:, k * H:(k + 1) * H], xn[:, b * NT + c * TPC + t, k * P:(k + 1) * P],
                                            A_sb[:, par, t * H:(t + 1) * H], start=(first and k == 0),
                                            stop=(c == NC - 1 and t == TPC - 1), skip_group_check=True)
            return last

        def pe_project(dst, wT, vec):
            for j in range(G):
                for k in range(G):
                    last = nc.tensor.matmul(dst[:, j, :], wT[:, k, j * P:(j + 1) * P],
                                            vec[:, k, j * HG:(j + 1) * HG], start=(k == 0), stop=(k == G - 1))
            return last

        def pe_w():
            for k in range(G):
                for j in range(G):
                    last = nc.tensor.matmul(ps_w[:, k, j * HG:(j + 1) * HG], wk_sb[:, j, k * P:(k + 1) * P],
                                            qsel[:, j, :], start=True, stop=True)
            return last

        def pe_score(slot):
            for g in range(G):
                last = nc.tensor.matmul(pS[0:H, :], w_sb[:, g, :], xT[:, slot, g, :],
                                        start=(g == 0), stop=(g == G - 1))
            return last

        s_const = sem("s_const")
        s_iota = sem("s_iota")
        s_steps = sem("s_steps")
        s_cond = sem("s_cond")
        s_condT = sem("s_condT")
        s_vinit = sem("s_vinit")
        s_tcol = sem("s_tcol")
        s_xin = [sem(f"s_xin{i}") for i in range(B * NC)]
        s_wt = sem("s_wt")
        s_wq = sem("s_wq")
        s_wk = sem("s_wk")
        s_wv = sem("s_wv")
        s_wo = sem("s_wo")
        s_mask = sem("s_mask")
        s_mrow = sem("s_mrow")
        s_out = sem("s_out")
        s_pin = sem("s_pin")
        s_rate = sem("s_rate")
        s_xT = sem("s_xT")
        s_tp = sem("s_tp")
        s_tpd = sem("s_tpd")
        s_Up = sem("s_Up")
        s_U = sem("s_U")
        s_x1T = sem("s_x1T")
        s_bk = sem("s_bk")
        s_bkout = sem("s_bkout")
        s_Ap = sem("s_Ap")
        s_A = sem("s_A")
        s_Yc = sem("s_Yc")
        s_y = sem("s_y")
        s_qp = sem("s_qp")
        s_q = sem("s_q")
        s_wp = sem("s_wp")
        s_w = sem("s_w")
        s_neg = sem("s_neg")
        s_sp = sem("s_sp")
        s_sc = sem("s_sc")
        s_mx = sem("s_mx")
        s_ex = sem("s_ex")
        s_pp = sem("s_pp")
        s_pT = sem("s_pT")
        s_zp = sem("s_zp")
        s_z = sem("s_z")
        s_op = sem("s_op")
        s_o = sem("s_o")
        s_yp = sem("s_yp")
        s_orow = sem("s_orow")
        s_add = sem("s_add")
        s_add2 = sem("s_add2")
        s_xor = sem("s_xor")
        s_xs = sem("s_xs")
        s_gd = sem("s_gd")
        s_vd = sem("s_vd")
        s_dve = sem("s_dve")

        ps_bad = pM[:, 312:313]
        s_badp = sem("s_badp")

        UNITS = B * NC * G

        with nc.Block() as block:
            @block.sync
            def _(sp):
                def load_x(b, c):
                    sp.dma_start(xn[:, b * NT + c * TPC:b * NT + (c + 1) * TPC, :],
                                 x_t[b, :, c * TPC:(c + 1) * TPC, :]).then_inc(s_xin[b * NC + c], 16)

                sp.dma_start(cond_rows[:, :], cond.rearrange("b (g p) -> (b g) p", p=P)).then_inc(s_cond, 16)
                load_x(0, 0)
                sp.dma_start(wstage, w_rows(wt)).then_inc(s_wt, 16)
                sp.dma_start(wq_sb[:, :, :], w_rows(wq)).then_inc(s_wq, 16)
                load_x(0, 1)
                sp.dma_start(row0, row0_words.to_broadcast([P, SEQ // 4])).then_inc(s_mrow, 16)
                sp.dma_start(mask0, mask[0:1, :].to_broadcast([H, SEQ])).then_inc(s_mrow, 16)
                sp.dma_start(wk_sb[:, :, :], w_rows(wk)).then_inc(s_wk, 16)
                sp.dma_start(masks, mask_words).then_inc(s_mask, 16)
                load_x(0, 2)
                load_x(0, 3)
                sp.wait_ge(s_bk, USE_WT + G)
                sp.dma_start(wstage, w_rows(wv)).then_inc(s_wv, 16)
                sp.wait_ge(s_bk, USE_WV + G)
                sp.dma_start(wstage, w_rows(wo)).then_inc(s_wo, 16)
                sp.wait_ge(s_xs, 1)
                for c in range(NC):
                    load_x(1, c)
                for b in range(B):
                    for q in range(NC):
                        if b == 0:
                            sp.wait_ge(s_add, (q + 1) * TPC)
                        else:
                            sp.wait_ge(s_add, NT + (q + 1) * TPC // 2)
                            sp.wait_ge(s_add2, (q + 1) * TPC // 2)
                        t0 = b * NT + q * TPC
                        sp.dma_start(out_t[b, :, q * TPC:(q + 1) * TPC, :], xn[:, t0:t0 + TPC, :]).then_inc(s_out, 16)
                sp.wait_ge(s_out, 16 * B * NC)

            @block.gpsimd
            def _(pool):
                nc.gpsimd.memset(ident[:, :], 0.0).then_inc(s_const, 1)
                pool.wait_ge(s_const, 1)
                nc.gpsimd.affine_select(out=ident[:, :], in_=ident[:, :], compare_op=ALU.not_equal, fill=1.0,
                                        base=0, pattern=[[-1, P]], channel_multiplier=1).then_inc(s_const, 1)
                nc.gpsimd.memset(ones[:, :], 1.0).then_inc(s_const, 1)
                nc.gpsimd.iota(steps_ii, pattern=[[1, CHUNK + 1]], base=0, channel_multiplier=0).then_inc(s_iota, 1)
                pool.wait_ge(s_iota, 1)
                nc.gpsimd.tensor_copy(steps, steps_ii).then_inc(s_steps, 1)
                nc.gpsimd.memset(headmask[:, :], 1.0).then_inc(s_const, 1)
                pool.wait_ge(s_const, 4)
                nc.gpsimd.affine_select(out=headmask[:, :], in_=headmask[:, :], compare_op=ALU.is_ge, fill=0.0,
                                        base=0, pattern=[[-E, HG]], channel_multiplier=1).then_inc(s_const, 1)
                pool.wait_ge(s_const, 5)
                nc.gpsimd.affine_select(out=headmask[:, :], in_=headmask[:, :], compare_op=ALU.is_gt, fill=0.0,
                                        base=E, pattern=[[E, HG]], channel_multiplier=-1).then_inc(s_const, 1)
                for b in range(B):
                    if b:
                        pool.wait_ge(s_pp, b)
                    else:
                        pool.wait_ge(s_xor, 1)
                    nc.gpsimd.memset(prob, NEG).then_inc(s_neg, 1)
                    pool.wait_ge(s_orow, b + 1)
                    for t in range(NT):
                        if b == 0 or t % 2 == 0:
                            nc.gpsimd.tensor_tensor(xn[:, b * NT + t, :], xn[:, b * NT + t, :], orow,
                                                    ALU.add).then_inc(s_add, 1)

            @block.scalar
            def _(act):
                def bank_evict(use, dst):
                    act.wait_ge(s_bk, use + 1)
                    nc.scalar.copy(dst, pbk[use % 2][:, :]).then_inc(s_bkout, 1)

                def weight_evict(dst, use):
                    for k in range(G):
                        bank_evict(use + k, dst[:, k, :])

                def unit_evict(b, c):
                    for g in range(G):
                        u = (b * NC + c) * G + g
                        act.wait_ge(s_pin, u + 1)
                        if u >= G:
                            act.wait_ge(s_x1T, u - G + 1)
                        nc.scalar.activation(rate2[:, g, :].rearrange("p (n two) -> p n two", two=2),
                                             pin[u % 2][:, :].unsqueeze(2).to_broadcast([P, CHUNK, 2]),
                                             ACT.Relu, scale=DT).then_inc(s_rate, 1)
                        if g == 0 and b * NC + c == SLOTS:
                            act.wait_ge(s_sp, NC)
                        if g == 0 and b * NC + c == SLOTS - 2:
                            act.wait_ge(s_tp, 1)
                        nc.scalar.copy(xT[:, chunk_slot(b, c), g, :], pin[u % 2][:, :]).then_inc(s_xT, 1)

                def back_evict(b, c):
                    for t in range(TPC):
                        bank_evict(use_back(b * NC + c) + t, xn[:, b * NT + c * TPC + t, :])
                    n = b * NC + c
                    act.wait_ge(s_Ap, n + 1)
                    if n >= 2:
                        act.wait_ge(s_Yc, n - 1)
                    nc.scalar.copy(A_sb[:, n % 2, :], pAP[:, 0:TPC * H]).then_inc(s_A, 1)

                def middle_scores(b):
                    act.wait_ge(s_Yc, NC * (b + 1))
                    nc.scalar.copy(y_sb[:, :, :], pY[:, 0:G * H].rearrange("p (k h) -> p k h", k=G)).then_inc(s_y, 1)
                    act.wait_ge(s_wp, b + 1)
                    nc.scalar.mul(w_sb[:, :, :], ps_w, SCALE).then_inc(s_w, 1)

                def middle_probs(b):
                    act.wait_ge(s_mx, b + 1)
                    nc.scalar.activation(prob, prob, ACT.Exp, bias=nmx[0:H, :]).then_inc(s_ex, 1)
                    act.wait_ge(s_pp, b + 1)
                    nc.scalar.copy(pT[:, :], pAP[:, 256:512]).then_inc(s_pT, 1)

                def middle_row(b):
                    act.wait_ge(s_yp, b + 1)
                    if b:
                        act.wait_ge(s_add, NT)
                    nc.scalar.copy(orow, pS[:, :]).then_inc(s_orow, 1)

                act.wait_ge(s_condT, 1)
                cols = pM[:, 0:B * G].rearrange("p (b g) -> p b g", b=B)
                nc.scalar.copy(vinit[:, :, :], cols).then_inc(s_vinit, 1)
                nc.scalar.copy(tcol[:, :, :], cols.rearrange("p b g -> p g b")).then_inc(s_tcol, 1)
                unit_evict(0, 0)
                weight_evict(wtT, USE_WT)
                weight_evict(wqT, USE_WQ)
                unit_evict(0, 1)
                weight_evict(wvT, USE_WV)
                back_evict(0, 0)
                act.wait_ge(s_xor, 1)
                nc.scalar.activation(masks_f, masks, ACT.Square, accum_out=xorsum[:, :]).then_inc(s_xs, 1)
                unit_evict(0, 2)
                weight_evict(woT, USE_WO)
                back_evict(0, 1)
                unit_evict(0, 3)
                back_evict(0, 2)
                unit_evict(1, 0)
                back_evict(0, 3)
                middle_scores(0)
                middle_probs(0)
                unit_evict(1, 1)
                middle_row(0)
                back_evict(1, 0)
                unit_evict(1, 2)
                back_evict(1, 1)
                unit_evict(1, 3)
                back_evict(1, 2)
                back_evict(1, 3)
                middle_scores(1)
                middle_probs(1)
                middle_row(1)

            @block.vector
            def _(dve):
                n = [0]

                def link(ins):
                    n[0] += 1
                    ins.then_inc(s_dve, 1)
                    dve.wait_ge(s_dve, n[0])

                def mark(ins):
                    n[0] += 1
                    ins.then_inc(s_dve, 1)

                def catch_up():
                    dve.wait_ge(s_dve, n[0])

                def pair(b, c, pr):
                    k = b * NC + c
                    gs = (2 * pr, 2 * pr + 1)
                    start = vinit[:, b, 2 * pr:2 * pr + 2] if c == 0 else vend[:, k - 1, 2 * pr:2 * pr + 2]
                    if c == 0 and pr == 0:
                        dve.wait_ge(s_vinit, 1)
                    link(nc.vector.tensor_copy(path[:, 2 * pr:2 * pr + 2, 1], start))
                    for g in gs:
                        dve.wait_ge(s_rate, k * G + g + 1)
                        mark(nc.vector.tensor_tensor_scan(path[:, g, 2:PATH], rate2[:, g, :], rate2[:, g, :],
                                                          path[:, g, 1:2], ALU.add, ALU.add))
                    catch_up()
                    for i, g in enumerate(gs):
                        mark(nc.vector.tensor_scalar(junk[:, 0:CHUNK], path[:, g, 3:PATH:2], 1.0, 0.0, ALU.is_lt,
                                                     ALU.add, accum_out=cnt[:, i:i + 1]))
                        catch_up()
                    for i, g in enumerate(gs):
                        mark(nc.vector.scalar_tensor_tensor(junk[:, 0:CHUNK], steps[:, 0:CHUNK], cnt[:, i:i + 1],
                                                            rate2[:, g, 0:2 * CHUNK:2], ALU.is_equal, ALU.mult,
                                                            accum_out=rstar[:, k, g:g + 1]))
                        catch_up()
                        mark(nc.vector.scalar_tensor_tensor(junk, steps, cnt[:, i:i + 1],
                                                            path[:, g, 1:PATH:2], ALU.is_equal, ALU.mult,
                                                            accum_out=vprev[:, i:i + 1]))
                        catch_up()
                        mark(nc.vector.scalar_tensor_tensor(
                            late[:, i, :].rearrange("p (n two) -> p n two", two=2),
                            path[:, g, 1:PATH - 2:2].unsqueeze(2).to_broadcast([P, CHUNK, 2]), 1.0,
                            rate2[:, g, :].rearrange("p (n two) -> p n two", two=2), ALU.is_ge, ALU.mult))
                    rs = rstar[:, k, 2 * pr:2 * pr + 2]
                    link(nc.vector.tensor_tensor(vpre[:, :], vprev[:, :], rs, ALU.add))
                    for _ in range(SUB - 1):
                        link(nc.vector.scalar_tensor_tensor(nvlt[:, :], vpre[:, :], 1.0, vpre[:, :], ALU.is_ge,
                                                            ALU.subtract))
                        link(nc.vector.tensor_tensor(vpre[:, :], rs, nvlt[:, :], ALU.subtract))
                    mark(nc.vector.scalar_tensor_tensor(nvlt[:, :], vpre[:, :], 1.0, vpre[:, :], ALU.is_ge,
                                                        ALU.subtract))
                    mark(nc.vector.tensor_scalar(spk[:, :], vpre[:, :], 1.0, PER_SPIKE, ALU.is_ge, ALU.mult))
                    catch_up()
                    link(nc.vector.tensor_scalar(vstar[:, :], nvlt[:, :], -1.0, None, ALU.mult))
                    for i, g in enumerate(gs):
                        mark(nc.vector.tensor_tensor_scan(late[:, i, :], late[:, i, :], late[:, i, :],
                                                          vstar[:, i:i + 1], ALU.add, ALU.add))
                    catch_up()
                    mark(nc.vector.tensor_copy(vend[:, k, 2 * pr:2 * pr + 2], late[:, :, 2 * CHUNK - 1]))
                    for i, g in enumerate(gs):
                        xs = xT[:, chunk_slot(b, c), g, :]
                        link(nc.vector.tensor_scalar(junk[:, 0:CHUNK], steps[:, 0:CHUNK], cnt[:, i:i + 1],
                                                     spk[:, i:i + 1], ALU.is_equal, ALU.mult))
                        dve.wait_ge(s_xT, k * G + g + 1)
                        nc.vector.tensor_tensor(xs, xs, junk[:, 0:CHUNK], ALU.add).then_inc(s_x1T, 1)
                        dve.wait_ge(s_x1T, k * G + g + 1)

                def time_vector():
                    dve.wait_ge(s_tp, 1)
                    dve.wait_ge(s_const, 6)
                    for b in range(B):
                        nc.vector.tensor_tensor(tpd[:, :, b, :],
                                                ps_tp[:, :, b].unsqueeze(2).to_broadcast([P, G, HG]), hm_b(),
                                                ALU.mult).then_inc(s_tpd, 1)
                    dve.wait_ge(s_Up, 1)
                    nc.vector.tensor_copy(U[:, :, :, :], ps_U).then_inc(s_U, 1)

                def compare_masks():
                    dve.wait_ge(s_mask, 16)
                    dve.wait_ge(s_mrow, 32)
                    rows = masks.rearrange("p (r w) -> p r w", r=NT)
                    nc.vector.tensor_tensor(rows, rows, row0.unsqueeze(1).to_broadcast([P, NT, SEQ // 4]),
                                            ALU.bitwise_xor).then_inc(s_xor, 1)

                def mid_q(b):
                    dve.wait_ge(s_qp, b + 1)
                    nc.vector.tensor_tensor(qsel[:, :, :], ps_q, hm_b(), ALU.mult).then_inc(s_q, 1)

                def mid_scores(b):
                    dve.wait_ge(s_neg, b + 1)
                    for c in range(NC):
                        dve.wait_ge(s_sp, b * NC + c + 1)
                        nc.vector.copy_predicated(prob[:, c * CHUNK:(c + 1) * CHUNK],
                                                  mask0[:, c * CHUNK:(c + 1) * CHUNK],
                                                  pS[0:H, :]).then_inc(s_sc, 1)
                    dve.wait_ge(s_sc, (b + 1) * NC)
                    link(nc.vector.reduce_max(mx[0:H, :], prob, AX))
                    nc.vector.tensor_scalar(nmx[0:H, :], mx[0:H, :], -1.0, None, ALU.mult).then_inc(s_mx, 1)

                def mid_z(b):
                    dve.wait_ge(s_zp, b + 1)
                    link(nc.vector.reciprocal(rinv[:, :], ps_sum))
                    nc.vector.tensor_tensor(z_sb[:, :, :], ps_z, rinv[:, :].unsqueeze(1).to_broadcast([P, G, H]),
                                            ALU.mult).then_inc(s_z, 1)

                def mid_o(b):
                    dve.wait_ge(s_op, b + 1)
                    link(nc.vector.tensor_tensor(osel[:, :, :], ps_o, hm_b(), ALU.mult))
                    nc.vector.reduce_sum(ocol[:, :], osel[:, :, :], AX).then_inc(s_o, 1)

                dve.wait_ge(s_steps, 1)
                mids = {(1, 0, 0): mid_q, (1, 0, 1): mid_scores, (1, 1, 0): mid_z, (1, 1, 1): mid_o}
                for b in range(B):
                    for c in range(NC):
                        for pr in range(G // 2):
                            pair(b, c, pr)
                            if (b, c, pr) == (0, 0, 0):
                                time_vector()
                            if (b, c, pr) == (0, 1, 0):
                                compare_masks()
                            if (b, c, pr) in mids:
                                mids[(b, c, pr)](0)
                link(nc.vector.tensor_scalar(junk[:, 0:B * G], vinit[:, :, :].rearrange("p b g -> p (b g)"), 1.0,
                                             None, ALU.is_lt))
                link(nc.vector.tensor_reduce(good[:, 0:1], junk[:, 0:B * G], AX, ALU.min))
                link(nc.vector.tensor_scalar(junk[:, 0:UNITS], rstar[:, :, :].rearrange("p k g -> p (k g)"), 1.0,
                                             None, ALU.is_lt))
                link(nc.vector.tensor_reduce(good[:, 1:2], junk[:, 0:UNITS], AX, ALU.min))
                link(nc.vector.tensor_scalar(junk[:, 0:UNITS], vend[:, :, :].rearrange("p k g -> p (k g)"), 1.0,
                                             None, ALU.is_lt))
                link(nc.vector.tensor_reduce(good[:, 2:3], junk[:, 0:UNITS], AX, ALU.min))
                link(nc.vector.tensor_reduce(goodall[:, :], good[:, :], AX, ALU.min))
                dve.wait_ge(s_xs, 1)
                nc.vector.scalar_tensor_tensor(goodall[:, :], xorsum[:, :], 0.0, goodall[:, :], ALU.is_equal,
                                               ALU.mult).then_inc(s_gd, 1)
                mid_q(1)
                mid_scores(1)
                mid_z(1)
                mid_o(1)
                dve.wait_ge(s_badp, 1)
                nc.vector.tensor_scalar(verdict[:, :], ps_bad, FORCE or P - 0.5, None,
                                        ALU.is_lt).then_inc(s_vd, 1)
                dve.wait_ge(s_orow, B)
                for t in range(1, NT, 2):
                    nc.vector.tensor_tensor(xn[:, NT + t, :], xn[:, NT + t, :], orow, ALU.add).then_inc(s_add2, 1)

            @block.tensor
            def _(pe):
                def bank_fill(use, src):
                    if use >= 2:
                        pe.wait_ge(s_bkout, use - 1)
                    return pe_transpose_tile(pbk[use % 2], src).then_inc(s_bk, 1)

                def weight(w, use):
                    for k in range(G):
                        bank_fill(use + k, [w[:, j, k * P:(k + 1) * P] for j in range(G)])

                def unit_in(b, c):
                    pe.wait_ge(s_xin[b * NC + c], 16)
                    for g in range(G):
                        u = (b * NC + c) * G + g
                        if u >= 2:
                            pe.wait_ge(s_xT, u - 1)
                        pe_transpose_tile(pin[u % 2], [xn[:, b * NT + c * TPC + t, g * P:(g + 1) * P]
                                                       for t in range(TPC)]).then_inc(s_pin, 1)

                def back(b, c):
                    k = b * NC + c
                    slot = chunk_slot(b, c)
                    pe.wait_ge(s_x1T, (k + 1) * G)
                    if k == 0:
                        pe.wait_ge(s_U, 1)
                    if k > 0:
                        pe.wait_ge(s_A, k)
                    pe_A(b, c, slot).then_inc(s_Ap, 1)
                    for t in range(TPC):
                        bank_fill(use_back(k) + t, [xT[:, slot, g, t * P:(t + 1) * P] for g in range(G)])
                    pe.wait_ge(s_A, k + 1)
                    pe.wait_ge(s_bkout, use_back(k) + TPC)
                    if k == NC:
                        pe.wait_ge(s_y, 1)
                    pe_Y(b, c, k % 2).then_inc(s_Yc, 1)

                def middle_scores(b):
                    pe.wait_ge(s_y, b + 1)
                    pe_project(ps_q, wqT, y_sb).then_inc(s_qp, 1)
                    pe.wait_ge(s_q, b + 1)
                    pe.wait_ge(s_wk, 16)
                    pe_w().then_inc(s_wp, 1)
                    pe.wait_ge(s_w, b + 1)
                    for c in range(NC):
                        if b * NC + c:
                            pe.wait_ge(s_sc, b * NC + c)
                        if c == 0 and b:
                            pe.wait_ge(s_orow, b)
                        pe_score(chunk_slot(b, c)).then_inc(s_sp, 1)

                def middle_probs(b):
                    pe.wait_ge(s_ex, b + 1)
                    if b:
                        pe.wait_ge(s_pT, b)
                    for t in range(NT):
                        last = nc.tensor.transpose(pAP[:, 256 + t * H:256 + (t + 1) * H],
                                                   prob[:, t * P:(t + 1) * P], ident[0:H, 0:H])
                    last.then_inc(s_pp, 1)
                    pe.wait_ge(s_pT, b + 1)
                    for t in range(NT):
                        nc.tensor.matmul(ps_sum, ones[:, :], pT[:, t * H:(t + 1) * H], start=(t == 0),
                                         stop=(t == NT - 1))
                    for t in range(NT):
                        for k in range(G):
                            last = nc.tensor.matmul(ps_z[:, k, :], xn[:, b * NT + t, k * P:(k + 1) * P],
                                                    pT[:, t * H:(t + 1) * H], start=(t == 0 and k == 0),
                                                    stop=(t == NT - 1), skip_group_check=True)
                    last.then_inc(s_zp, 1)

                def middle_row(b):
                    pe.wait_ge(s_z, b + 1)
                    pe_project(ps_o, wvT, z_sb).then_inc(s_op, 1)
                    pe.wait_ge(s_o, b + 1)
                    for j in range(G):
                        last = nc.tensor.matmul(pS[:, :], ocol[:, j:j + 1].to_broadcast([P, P]), woT[:, j, :], start=(j == 0),
                                                stop=(j == G - 1))
                    last.then_inc(s_yp, 1)

                pe.wait_ge(s_const, 6)
                pe.wait_ge(s_cond, 16)
                nc.tensor.transpose(pM[:, 0:B * G], cond_rows[:, :], ident[0:B * G, 0:B * G]).then_inc(s_condT, 1)
                unit_in(0, 0)
                pe.wait_ge(s_wt, 16)
                weight(wstage, USE_WT)
                pe.wait_ge(s_wq, 16)
                weight(wq_sb, USE_WQ)
                pe.wait_ge(s_bkout, USE_WT + G)
                pe.wait_ge(s_tcol, 1)
                for j in range(G):
                    for k in range(G):
                        last = nc.tensor.matmul(ps_tp[:, j, :], wtT[:, k, j * P:(j + 1) * P], tcol[:, k, :],
                                                start=(k == 0), stop=(k == G - 1))
                last.then_inc(s_tp, 1)
                pe.wait_ge(s_tpd, B)
                for k in range(G):
                    for j in range(G):
                        last = nc.tensor.matmul(ps_U[:, k, :, j * HG:(j + 1) * HG], wq_sb[:, j, k * P:(k + 1) * P],
                                                tpd[:, j, :, :], start=True, stop=True)
                last.then_inc(s_Up, 1)
                unit_in(0, 1)
                pe.wait_ge(s_wv, 16)
                weight(wstage, USE_WV)
                back(0, 0)
                unit_in(0, 2)
                pe.wait_ge(s_wo, 16)
                weight(wstage, USE_WO)
                back(0, 1)
                unit_in(0, 3)
                back(0, 2)
                unit_in(1, 0)
                back(0, 3)
                middle_scores(0)
                middle_probs(0)
                unit_in(1, 1)
                middle_row(0)
                back(1, 0)
                unit_in(1, 2)
                back(1, 1)
                unit_in(1, 3)
                back(1, 2)
                pe.wait_ge(s_gd, 1)
                nc.tensor.matmul(ps_bad, ones[:, :], goodall[:, :], start=True, stop=True).then_inc(s_badp, 1)
                back(1, 3)
                middle_scores(1)
                middle_probs(1)
                middle_row(1)

        sc = cut(SEQ, True)[0:H, :]
        sel = cut(H * P)[0:H, :]
        onehot = cut(P)[0:H, :]
        mrows = cut(SEQ // 4).bitcast(u8)
        S = cut(SEQ)
        ST = cut(SEQ)
        O = cut(D)
        OT = cut(D).rearrange("p (j n) -> p j n", j=G)
        res = cut(D)
        tile = cut(D).rearrange("p (g n) -> p g n", g=G)
        v, r, a, m, n0, f = [cut(G).rearrange("p (g n) -> p g n", g=G) for _ in range(6)]
        rowmax, nrowmax, rowsum, rrow = [cut(1) for _ in range(4)]
        pscore = [pin[0], pin[1], pbk[0], pbk[1]]
        pturn = [pAP, pY, pS, pM]

        g_sel = sem("g_sel")
        g_ld = sem("g_ld")
        g_tp = sem("g_tp")
        g_ev = sem("g_ev")
        g_bt = sem("g_bt")
        g_btp = sem("g_btp")
        g_bev = sem("g_bev")
        g_A = sem("g_A")
        g_Ae = sem("g_Ae")
        g_Y = sem("g_Y")
        g_ye = sem("g_ye")
        g_q = sem("g_q")
        g_qe = sem("g_qe")
        g_w = sem("g_w")
        g_we = sem("g_we")
        g_s = sem("g_s")
        g_se = sem("g_se")
        g_v = sem("g_v")
        g_ve = sem("g_ve")
        g_mk = sem("g_mk")
        g_neg = sem("g_neg")
        g_oh = sem("g_oh")
        g_bc = sem("g_bc")
        g_cp = sem("g_cp")
        g_mx = sem("g_mx")
        g_ex = sem("g_ex")
        g_st = sem("g_st")
        g_ste = sem("g_ste")
        g_o = sem("g_o")
        g_O = sem("g_O")
        g_ot = sem("g_ot")
        g_ote = sem("g_ote")
        g_y = sem("g_y")
        g_res = sem("g_res")
        g_out = sem("g_out")
        g_dve = sem("g_dve")
        g_go = sem("g_go")
        g_sum = sem("g_sum")


        with nc.Block() as block:
            @block.sync
            def _(sp):
                bad = sp.value_load(verdict[0:1, 0:1])
                with sp.If(bad > 0):
                    sp.sem_inc(g_out, 16)
                    for b in range(B):
                        with sp.Fori(0, NT) as t:
                            sp.wait_ge(g_tp, t + (b * NT + 1))
                            sp.dma_start(tile, x_t[b, :, bass.ds(t, 1), :]
                                         .rearrange("p t (g n) -> p (t g) n", g=G)).then_inc(g_ld, 16)
                        with sp.Fori(0, NT) as t:
                            sp.wait_ge(g_res, t + (b * NT + 1))
                            sp.dma_start(mrows, mask[bass.ds(t * P, P), :]).then_inc(g_mk, 16)
                            sp.wait_ge(g_res, t + (b * NT + 2))
                            sp.dma_start(out_t[b, :, bass.ds(t, 1), :],
                                         res.unsqueeze(1)).then_inc(g_out, 16)
                    sp.wait_ge(g_out, 16 * (B * NT + 1))
                sp.end_ifs()

            @block.gpsimd
            def _(pool):
                bad = pool.value_load(verdict[0:1, 0:1])
                with pool.If(bad > 0):
                    nc.gpsimd.memset(sel, 1.0).then_inc(g_sel, 1)
                    pool.wait_ge(g_sel, 1)
                    nc.gpsimd.affine_select(out=sel, in_=sel, compare_op=ALU.is_ge, fill=0.0, base=0,
                                            pattern=[[1, H * P]], channel_multiplier=-P).then_inc(g_sel, 1)
                    pool.wait_ge(g_sel, 2)
                    nc.gpsimd.affine_select(out=sel, in_=sel, compare_op=ALU.is_gt, fill=0.0, base=P,
                                            pattern=[[-1, H * P]], channel_multiplier=P).then_inc(g_sel, 1)
                    with pool.Fori(0, B * NT * H) as i:
                        pool.wait_ge(g_st, i + 1)
                        pool.sem_inc(g_go, 1)
                        nc.gpsimd.memset(S, NEG).then_inc(g_neg, 1)
                pool.end_ifs()

            @block.scalar
            def _(act):
                bad = act.value_load(verdict[0:1, 0:1])
                with act.If(bad > 0):
                    act.sem_inc(g_ev, 1)
                    act.sem_inc(g_bev, 1)
                    for b in range(B):
                        with act.Fori(0, NC) as c:
                            with act.Fori(0, TPC) as t:
                                act.wait_ge(g_tp, c * TPC + t + (b * NT + 2))
                                nc.scalar.copy(xT[:, bass.ds(c, 1), :, bass.ds(t * P, P)],
                                               pin[0][:, :].rearrange("p (g n) -> p g n", g=G).unsqueeze(1)).then_inc(g_ev, 1)
                        with act.Fori(0, NT) as t:
                            act.wait_ge(g_btp, t + (b * NT + 2))
                            nc.scalar.copy(xn[:, bass.ds(t + b * NT, 1), :], pin[1][:, :].unsqueeze(1)).then_inc(g_bev, 1)
                        for c in range(NC):
                            k = b * NC + c
                            act.wait_ge(g_A, k + 1)
                            nc.scalar.copy(A_sb[:, 0, :], pAP[:, 0:TPC * H]).then_inc(g_Ae, 1)
                        act.wait_ge(g_Y, NC * (b + 1))
                        nc.scalar.copy(y_sb[:, :, :], pY[:, 0:G * H].rearrange("p (k h) -> p k h", k=G)).then_inc(g_ye, 1)
                        act.wait_ge(g_w, b + 1)
                        nc.scalar.mul(w_sb[:, :, :], ps_w, SCALE).then_inc(g_we, 1)
                        for c in range(NC):
                            k = b * NC + c
                            act.wait_ge(g_s, k + 1)
                            nc.scalar.copy(sc[:, c * CHUNK:(c + 1) * CHUNK], pS[0:H, :]).then_inc(g_se, 1)
                        for t in range(NT):
                            i = b * NT + t
                            act.wait_ge(g_v, i + 1)
                            nc.scalar.copy(xT[:, t // TPC, :, (t % TPC) * P:(t % TPC + 1) * P],
                                           pbk[t % 2][:, :].rearrange("p (g n) -> p g n", g=G)).then_inc(g_ve, 1)
                        with act.Fori(0, NT) as t:
                            with act.Fori(0, H) as h:
                                i = t * H + h
                                act.wait_ge(g_mx, i + (b * NT * H + 1))
                                nc.scalar.activation(S, S, ACT.Exp, bias=nrowmax, accum_out=rowsum).then_inc(g_ex, 1)
                                act.wait_ge(g_st, i + (b * NT * H + 2))
                                for q in range(NC):
                                    nc.scalar.copy(ST[:, q * CHUNK:(q + 1) * CHUNK], pturn[q][:, :]).then_inc(g_ste, 1)
                            act.wait_ge(g_ot, t + (b * NT + 1))
                            nc.scalar.copy(OT, pin[1][:, :].rearrange("p (j n) -> p j n", j=G)).then_inc(g_ote, 1)
                act.end_ifs()

            @block.vector
            def _(dve):
                bad = dve.value_load(verdict[0:1, 0:1])
                with dve.If(bad > 0):
                    dve.sem_inc(g_res, 1)
                    dve.wait_ge(g_sel, 3)
                    OPS = 1 + SUB * 7 + 2
                    for b in range(B):
                        dve.wait_ge(g_ev, NT * (b + 1) + 1)
                        nc.vector.tensor_copy(v, vinit[:, b, :].unsqueeze(2)).then_inc(g_dve, 1)
                        with dve.Fori(0, NC) as c:
                            with dve.Fori(0, CHUNK) as s:
                                before = (c * CHUNK + s) * OPS + (b * (SEQ * OPS + 1) + 1)
                                done = [0]

                                def link(ins):
                                    ins.then_inc(g_dve, 1)
                                    done[0] += 1
                                    dve.wait_ge(g_dve, before + done[0])

                                xs = xT[:, bass.ds(c, 1), :, bass.ds(s, 1)].rearrange("p c g n -> p (c g) n")
                                dve.wait_ge(g_dve, before)
                                link(nc.vector.tensor_scalar(r, xs, 0.0, DT, ALU.max, ALU.mult))
                                for _ in range(SUB):
                                    link(nc.vector.tensor_tensor(a, v, r, ALU.add))
                                    link(nc.vector.tensor_scalar(m, a, TWO23, TWO23, ALU.min, ALU.add))
                                    link(nc.vector.tensor_scalar(n0, m, TWO23, None, ALU.subtract))
                                    link(nc.vector.tensor_tensor(f, n0, a, ALU.is_gt))
                                    link(nc.vector.tensor_tensor(n0, n0, f, ALU.subtract))
                                    link(nc.vector.tensor_tensor(v, a, n0, ALU.subtract))
                                    link(nc.vector.scalar_tensor_tensor(v, a, TWO23, v, ALU.is_lt, ALU.mult))
                                link(nc.vector.tensor_tensor(a, a, v, ALU.subtract))
                                link(nc.vector.scalar_tensor_tensor(xs, a, PER_SPIKE, xs, ALU.mult, ALU.add))
                                assert done[0] == OPS
                        dve.wait_ge(g_dve, (b + 1) * (SEQ * OPS + 1))
                        with dve.Fori(0, NC) as c:
                            with dve.Fori(0, TPC) as t:
                                dve.wait_ge(g_btp, c * TPC + t + (b * NT + 1))
                                nc.vector.tensor_copy(tile, xT[:, bass.ds(c, 1), :, bass.ds(t * P, P)]
                                                      .rearrange("p c g n -> p (c g) n")).then_inc(g_bt, 1)
                        dve.wait_ge(g_q, b + 1)
                        nc.vector.tensor_tensor(qsel[:, :, :], ps_q, hm_b(), ALU.mult).then_inc(g_qe, 1)
                        with dve.Fori(0, NT) as t:
                            with dve.Fori(0, H) as h:
                                i = t * H + h
                                dve.wait_ge(g_mk, (t + (b * NT + 1)) * 16)
                                nc.vector.tensor_copy(onehot, sel[:, bass.ds(h * P, P)]).then_inc(g_oh, 1)
                                dve.wait_ge(g_neg, i + (b * NT * H + 1))
                                dve.wait_ge(g_bc, i + (b * NT * H + 1))
                                dve.sem_inc(g_go, 1)
                                for q in range(NC):
                                    cs = slice(q * CHUNK, (q + 1) * CHUNK)
                                    nc.vector.copy_predicated(S[:, cs], mrows[:, cs], pscore[q][:, :]).then_inc(g_cp, 1)
                                dve.wait_ge(g_cp, (i + (b * NT * H + 1)) * NC)
                                nc.vector.reduce_max(rowmax, S, AX).then_inc(g_sum, 1)
                                dve.wait_ge(g_sum, i * 2 + (b * NT * H * 2 + 1))
                                nc.vector.tensor_scalar(nrowmax, rowmax, -1.0, None, ALU.mult).then_inc(g_mx, 1)
                                dve.wait_ge(g_o, i + (b * NT * H + 1))
                                nc.vector.reciprocal(rrow, rowsum).then_inc(g_sum, 1)
                                dve.wait_ge(g_sum, i * 2 + (b * NT * H * 2 + 2))
                                nc.vector.tensor_scalar(O[:, bass.ds(h * E, E)], pin[0][:, 0:E], rrow, None,
                                                        ALU.mult).then_inc(g_O, 1)
                            dve.wait_ge(g_y, t + (b * NT + 1))
                            dve.wait_ge(g_out, (t + (b * NT + 1)) * 16)
                            nc.vector.tensor_tensor(res.unsqueeze(1), pbk[0][:, :].unsqueeze(1),
                                                    xn[:, bass.ds(t + b * NT, 1), :], ALU.add).then_inc(g_res, 1)
                dve.end_ifs()

            @block.tensor
            def _(pe):
                bad = pe.value_load(verdict[0:1, 0:1])
                with pe.If(bad > 0):
                    pe.sem_inc(g_tp, 1)
                    pe.sem_inc(g_btp, 1)
                    pe.sem_inc(g_st, 1)
                    for b in range(B):
                        with pe.Fori(0, NT) as t:
                            pe.wait_ge(g_ld, (t + (b * NT + 1)) * 16)
                            pe.wait_ge(g_ev, t + (b * NT + 1))
                            pe_transpose_tile(pin[0], [tile[:, g, :] for g in range(G)]).then_inc(g_tp, 1)
                        with pe.Fori(0, NT) as t:
                            pe.wait_ge(g_bt, t + (b * NT + 1))
                            pe.wait_ge(g_bev, t + (b * NT + 1))
                            pe_transpose_tile(pin[1], [tile[:, g, :] for g in range(G)]).then_inc(g_btp, 1)
                        pe.wait_ge(g_bev, NT * (b + 1) + 1)
                        for c in range(NC):
                            k = b * NC + c
                            pe_A(b, c, c).then_inc(g_A, 1)
                            pe.wait_ge(g_Ae, k + 1)
                            pe_Y(b, c, 0).then_inc(g_Y, 1)
                        pe.wait_ge(g_ye, b + 1)
                        pe_project(ps_q, wqT, y_sb).then_inc(g_q, 1)
                        pe.wait_ge(g_qe, b + 1)
                        pe_w().then_inc(g_w, 1)
                        pe.wait_ge(g_we, b + 1)
                        for c in range(NC):
                            if b * NC + c:
                                pe.wait_ge(g_se, b * NC + c)
                            pe_score(c).then_inc(g_s, 1)
                        for t in range(NT):
                            i = b * NT + t
                            if i >= 2:
                                pe.wait_ge(g_ve, i - 1)
                            for g in range(G):
                                last = nc.tensor.matmul(pbk[t % 2][:, :],
                                                        xT[:, t // TPC, g, (t % TPC) * P:(t % TPC + 1) * P],
                                                        wvT[:, g, :], start=(g == 0), stop=(g == G - 1))
                            last.then_inc(g_v, 1)
                        pe.wait_ge(g_ve, NT * (b + 1))
                        pe.wait_ge(g_se, NC * (b + 1))
                        with pe.Fori(0, NT) as t:
                            with pe.Fori(0, G) as hg:
                                with pe.Fori(0, HG) as hh:
                                    i = t * H + hg * HG + hh
                                    pe.wait_ge(g_oh, i + (b * NT * H + 1))
                                    for q in range(NC):
                                        last = nc.tensor.matmul(pscore[q][:, :], onehot,
                                                                sc[:, q * CHUNK:(q + 1) * CHUNK], start=True, stop=True)
                                    last.then_inc(g_bc, 1)
                                    pe.wait_ge(g_ex, i + (b * NT * H + 1))
                                    for q in range(NC):
                                        last = pe_transpose_tile(pturn[q], [S[:, (q * TPC + n) * P:(q * TPC + n + 1) * P]
                                                                            for n in range(TPC)])
                                    last.then_inc(g_st, 1)
                                    pe.wait_ge(g_ste, (i + (b * NT * H + 1)) * NC)
                                    for n in range(NT):
                                        vh = xT[:, n // TPC, bass.ds(hg, 1), bass.ds(hh * E + (n % TPC) * P, E)]
                                        last = nc.tensor.matmul(pin[0][:, 0:E], ST[:, n * P:(n + 1) * P],
                                                                vh.rearrange("p g n -> p (g n)"),
                                                                start=(n == 0), stop=(n == NT - 1))
                                    last.then_inc(g_o, 1)
                            pe.wait_ge(g_O, (t + (b * NT + 1)) * H)
                            pe_transpose_tile(pin[1], [O[:, j * P:(j + 1) * P] for j in range(G)]).then_inc(g_ot, 1)
                            pe.wait_ge(g_ote, t + (b * NT + 1))
                            for j in range(G):
                                last = nc.tensor.matmul(pbk[0][:, :], OT[:, j, :], woT[:, j, :], start=(j == 0),
                                                        stop=(j == G - 1))
                            last.then_inc(g_y, 1)
                pe.end_ifs()


_INS = ['x', 'cond_1024', 'mask_SxS_bk0', 'L1_cond_Wq', 'L1_cond_Wk', 'L1_cond_Wv', 'L1_cond_Wt', 'L1_cond_Wo']
_OUTS = [((2, 2048, 512), 'float32')]


def kernel(**inputs):
    import numpy as _np
    import concourse.bacc as _bacc
    from concourse import mybir as _mybir
    from concourse.bass_utils import run_bass_kernel_spmd as _run

    nc = _bacc.Bacc("TRN2", target_bir_lowering=False, num_devices=1)
    arrays, args = {}, []
    for name in _INS:
        a = _np.ascontiguousarray(inputs[name])
        arrays[f"in_{name}_dram"] = a
        args.append(nc.dram_tensor(f"in_{name}_dram", a.shape, _mybir.dt.from_np(a.dtype), kind="ExternalInput").ap())
    for i, (shape, dtype) in enumerate(_OUTS):
        dt = _mybir.dt.from_np(_np.dtype(dtype))
        args.append(nc.dram_tensor(f"out_{i}_dram", shape, dt, kind="ExternalOutput").ap())
    spiking_residual_attention(nc, *args)
    r = _run(nc, [arrays], core_ids=[0])
    got = tuple(r.results[0][f"out_{i}_dram"] for i in range(len(_OUTS)))
    return got[0]
```

```python
import concourse.bass as bass
from concourse import mybir
from contextlib import ExitStack


def spiking_residual_attention(nc, x, cond, mask, wq, wk, wv, wt, wo, out, FORCE=None):
    fp32 = mybir.dt.float32
    i32 = mybir.dt.int32
    u8 = mybir.dt.uint8
    ALU = mybir.AluOpType
    ACT = mybir.ActivationFunctionType
    AX = mybir.AxisListType.X

    B, SEQ, D = x.shape
    H = 16
    E = D // H
    P = 128
    G = D // P
    SUB = 4
    CHUNK = 512
    NC = SEQ // CHUNK
    TPC = CHUNK // P
    NT = SEQ // P
    HG = P // E
    SLAB = 32
    SLOTS = NC + 1
    DT = 0.001
    PER_SPIKE = 999.99993896484375
    SCALE = float(E) ** -0.5
    NEG = -3.4028234663852886e38
    ARENA = 12950
    TWO23 = 8388608.0

    x_t = x.rearrange("b (t p) d -> b p t d", p=P)
    out_t = out.rearrange("b (t p) d -> b p t d", p=P)
    mask_words = mask.rearrange("(p r) s -> p (r s)", p=P).bitcast(i32)
    row0_words = mask[0:1, :].bitcast(i32)

    def w_rows(w):
        return w.rearrange("(j p) d -> p j d", p=P)

    ctx = ExitStack()
    with ctx:
        def sb(name, shape, dt=fp32):
            return ctx.enter_context(nc.sbuf_tensor(name, shape, dt))

        def pb(name):
            return ctx.enter_context(nc.psum_tensor(name, [P, 512], fp32))

        def sem(name):
            return ctx.enter_context(nc.semaphore(name))

        xn = sb("xn", [P, B * NT, D])
        xT = sb("xT", [P, SLOTS, G, CHUNK])
        wq_sb = sb("wq_sb", [P, G, D])
        wk_sb = sb("wk_sb", [P, G, D])
        wqT = sb("wqT", [P, G, D])
        wvT = sb("wvT", [P, G, D])
        woT = sb("woT", [P, G, D])
        ident = sb("ident", [P, P])
        ones = sb("ones", [P, 1])
        headmask = sb("headmask", [P, SLAB])
        same = sb("same", [P, SLAB])
        same_all = sb("same_all", [P, G, SLAB])
        U = sb("U", [P, G, B, SLAB])
        tcol = sb("tcol", [P, G, B])
        tpd = sb("tpd", [P, G, B, HG])
        A_rows = sb("A_rows", [P, P])
        A_sb = sb("A_sb", [P, 2, TPC, SLAB])
        rows = sb("rows", [P, D])
        he_rows = sb("he_rows", [P, P])
        vec = sb("vec", [P, G, G, SLAB])
        qsel = sb("qsel", [P, G, SLAB])
        w_sb = sb("w_sb", [P, G, SLAB])
        pT = sb("pT", [P, TPC, P])
        mx = sb("mx", [P, 1])
        nmx = sb("nmx", [P, 1])
        mrow = rows[0:1, P:P + SLAB]
        mrow_all = rows[0:1, 0:P].rearrange("o (c h) -> o c h", c=G)
        part = sb("part", [P, 1])
        psum_rows = sb("psum_rows", [P, 1])
        share = sb("share", [P, 1])
        rtot = sb("rtot", [P, 1])
        comb = sb("comb", [P, SLAB])
        osel = sb("osel", [P, G, SLAB])
        ocol = sb("ocol", [P, G])
        vinit = sb("vinit", [P, B, G])
        rstar = sb("rstar", [P, B * NC, G])
        vend = sb("vend", [P, B * NC, G])
        cnt = sb("cnt", [P, 2])
        vprev = sb("vprev", [P, 2])
        vpre = sb("vpre", [P, 2])
        nvlt = sb("nvlt", [P, 2])
        vstar = sb("vstar", [P, 2])
        spk = sb("spk", [P, 2])
        good = sb("good", [P, 3])
        goodall = sb("goodall", [P, 1])
        xorsum = sb("xorsum", [P, 1])
        verdict = sb("verdict", [P, 1], i32)
        arena = sb("arena", [P, ARENA])
        at = [0]

        def cut(n, fresh=False):
            if fresh:
                at[0] = 0
            at[0] += n
            assert at[0] <= ARENA
            return arena[:, at[0] - n:at[0]]

        rate2 = cut(G * 2 * CHUNK, True).rearrange("p (g n) -> p g n", g=G)
        PATH = 2 * CHUNK + 2
        path = cut(G * PATH).rearrange("p (g n) -> p g n", g=G)
        late = cut(2 * 2 * CHUNK).rearrange("p (g n) -> p g n", g=2)
        steps = cut(CHUNK + 1)
        spikes = cut(2 * CHUNK).rearrange("p (g n) -> p g n", g=2)
        prob = cut(CHUNK)
        cond_rows = prob[0:B * G, 0:P]
        orow = cut(D)
        row0 = orow.bitcast(i32)
        steps_ii = late[:, 0, 0:CHUNK + 1].bitcast(i32)
        mask0 = cut(CHUNK // 4).bitcast(u8)
        wstage = xT[:, SLOTS - 1, :, :]
        wtT = xT[:, SLOTS - 2, :, :]
        masks = xn[:, NT:2 * NT, :].rearrange("p t d -> p (t d)").bitcast(i32)
        masks_f = xn[:, NT:2 * NT, :].rearrange("p t d -> p (t d)")

        pin = [pb("pin0"), pb("pin1")]
        pbk = [pb("pbk0"), pb("pbk1")]
        pAP = pb("pAP")
        pY = pb("pY")
        pS = pb("pS")
        pM = pb("pM")
        ps_tp = pM[:, 0:8].rearrange("p (j b) -> p j b", b=B)
        ps_U = pM[:, 8:136].rearrange("p (k b h) -> p k b h", k=G, b=B)
        ps_q = pM[:, 136:152].rearrange("p (j h) -> p j h", j=G)
        ps_w = pM[:, 152:216].rearrange("p (k h) -> p k h", k=G)
        ps_rows = pM[:, 0:P]
        ps_cols = pM[:, P:2 * P].rearrange("p (j h) -> p j h", j=G)
        ps_comb = pM[:, 256:384].rearrange("p (k h) -> p k h", k=G)
        ps_mrow = pM[0:1, 384:512]
        ps_mcol = pAP[:, 384:385]
        ps_tot = pAP[:, 385:386]
        ps_bad = pAP[:, 386:387]

        def chunk_slot(b, c):
            return (b * NC + c) % SLOTS

        USE_WT, USE_WQ, USE_WV, USE_WO = 0, G, 2 * G, 3 * G + TPC

        def use_back(k):
            return 3 * G if k == 0 else 4 * G + k * TPC

        def hm_b():
            return headmask[:, 0:HG].unsqueeze(1).to_broadcast([P, G, HG])

        def hm_slab():
            return headmask[:, :].unsqueeze(1).to_broadcast([P, G, SLAB])

        def pe_transpose_tile(dst, src):
            for i, s in enumerate(src):
                last = nc.tensor.transpose(dst[:, i * P:(i + 1) * P], s, ident[:, :])
            return last

        def slab(i):
            return slice(i * SLAB, (i + 1) * SLAB)

        def pe_A(b, slot):
            for g in range(G):
                for t in range(TPC):
                    last = nc.tensor.matmul(pAP[slab(t), 0:P], U[:, g, b, :], xT[:, slot, g, t * P:(t + 1) * P],
                                            start=(g == 0), stop=(g == G - 1))
            return last

        def pe_Y(b, c, par):
            for t in range(TPC):
                last = nc.tensor.matmul(pY[slab(t), :], A_sb[:, par, t, :], xn[:, b * NT + c * TPC + t, :],
                                        start=(c == 0), stop=(c == NC - 1), skip_group_check=True)
            return last

        def pe_combine(by):
            for k in range(G):
                last = nc.tensor.matmul(ps_comb[:, k, :], rows[:, k * P:(k + 1) * P], by, start=True, stop=True)
            return last

        def pe_heads(wT):
            for k in range(G):
                for j in range(G):
                    last = nc.tensor.matmul(ps_rows[slab(j), :], vec[:, k, j, :], wT[:, k, j * P:(j + 1) * P],
                                            start=(k == 0), stop=(k == G - 1))
            return last

        def pe_w():
            for j in range(G):
                last = nc.tensor.matmul(pY[slab(j), :], qsel[:, j, :], wk_sb[:, j, :], start=True, stop=True)
            return last

        def pe_scores(b):
            for g in range(G):
                for c in range(NC):
                    last = nc.tensor.matmul(pS[slab(c), :], w_sb[:, g, :], xT[:, chunk_slot(b, c), g, :],
                                            start=(g == 0), stop=(g == G - 1))
            return last

        def pe_z(b):
            for t in range(TPC):
                for c in range(NC):
                    last = nc.tensor.matmul(pS[slab(c), :], pT[:, t, slab(c)], xn[:, b * NT + c * TPC + t, :],
                                            start=(t == 0), stop=(t == TPC - 1))
            return last

        s_const = sem("s_const")
        s_iota = sem("s_iota")
        s_steps = sem("s_steps")
        s_cond = sem("s_cond")
        s_condT = sem("s_condT")
        s_vinit = sem("s_vinit")
        s_tcol = sem("s_tcol")
        s_xin = [sem(f"s_xin{i}") for i in range(B * NC)]
        s_wt = sem("s_wt")
        s_wq = sem("s_wq")
        s_wk = sem("s_wk")
        s_wv = sem("s_wv")
        s_wo = sem("s_wo")
        s_mask = sem("s_mask")
        s_mrow = sem("s_mrow")
        s_out = sem("s_out")
        s_pin = sem("s_pin")
        s_rate = sem("s_rate")
        s_xT = sem("s_xT")
        s_tp = sem("s_tp")
        s_tpd = sem("s_tpd")
        s_Up = sem("s_Up")
        s_U = sem("s_U")
        s_x1T = sem("s_x1T")
        s_bk = sem("s_bk")
        s_bkout = sem("s_bkout")
        s_Ar = sem("s_Ar")
        s_Are = sem("s_Are")
        s_Ap = sem("s_Ap")
        s_A = sem("s_A")
        s_Yc = sem("s_Yc")
        s_Ye = sem("s_Ye")
        s_yc = sem("s_yc")
        s_y = sem("s_y")
        s_qp = sem("s_qp")
        s_qe = sem("s_qe")
        s_qt = sem("s_qt")
        s_q = sem("s_q")
        s_wp = sem("s_wp")
        s_wr = sem("s_wr")
        s_wtr = sem("s_wtr")
        s_w = sem("s_w")
        s_neg = sem("s_neg")
        s_sp = sem("s_sp")
        s_sc = sem("s_sc")
        s_mx = sem("s_mx")
        s_mt = sem("s_mt")
        s_mr = sem("s_mr")
        s_mb = sem("s_mb")
        s_f = sem("s_f")
        s_sh = sem("s_sh")
        s_tot = sem("s_tot")
        s_cb = sem("s_cb")
        s_ex = sem("s_ex")
        s_pp = sem("s_pp")
        s_pT = sem("s_pT")
        s_zp = sem("s_zp")
        s_ze = sem("s_ze")
        s_zc = sem("s_zc")
        s_z = sem("s_z")
        s_op = sem("s_op")
        s_oe = sem("s_oe")
        s_ot = sem("s_ot")
        s_o = sem("s_o")
        s_same = sem("s_same")
        s_spk = sem("s_spk")
        s_yp = sem("s_yp")
        s_orow = sem("s_orow")
        s_add = sem("s_add")
        s_add2 = sem("s_add2")
        s_xor = sem("s_xor")
        s_xs = sem("s_xs")
        s_gd = sem("s_gd")
        s_vd = sem("s_vd")
        s_dve = sem("s_dve")

        s_badp = sem("s_badp")

        UNITS = B * NC * G

        with nc.Block() as block:
            @block.sync
            def _(sp):
                def load_x(b, c):
                    sp.dma_start(xn[:, b * NT + c * TPC:b * NT + (c + 1) * TPC, :],
                                 x_t[b, :, c * TPC:(c + 1) * TPC, :]).then_inc(s_xin[b * NC + c], 16)

                sp.dma_start(cond_rows, cond.rearrange("b (g p) -> (b g) p", p=P)).then_inc(s_cond, 16)
                load_x(0, 0)
                sp.dma_start(wstage, w_rows(wt)).then_inc(s_wt, 16)
                sp.dma_start(wq_sb[:, :, :], w_rows(wq)).then_inc(s_wq, 16)
                load_x(0, 1)
                sp.dma_start(row0, row0_words.to_broadcast([P, SEQ // 4])).then_inc(s_mrow, 16)
                for c in range(NC):
                    sp.dma_start(mask0[slab(c), :], mask[0:1, c * CHUNK:(c + 1) * CHUNK]
                                 .to_broadcast([SLAB, CHUNK])).then_inc(s_mrow, 16)
                sp.dma_start(wk_sb[:, :, :], w_rows(wk)).then_inc(s_wk, 16)
                sp.dma_start(masks, mask_words).then_inc(s_mask, 16)
                load_x(0, 2)
                load_x(0, 3)
                sp.wait_ge(s_bk, USE_WT + G)
                sp.dma_start(wstage, w_rows(wv)).then_inc(s_wv, 16)
                sp.wait_ge(s_bk, USE_WV + G)
                sp.dma_start(wstage, w_rows(wo)).then_inc(s_wo, 16)
                sp.wait_ge(s_xs, 1)
                for c in range(NC):
                    load_x(1, c)
                for b in range(B):
                    for q in range(NC):
                        if b == 0:
                            sp.wait_ge(s_add, (q + 1) * TPC)
                        else:
                            sp.wait_ge(s_add, NT + (q + 1) * TPC // 2)
                            sp.wait_ge(s_add2, (q + 1) * TPC // 2)
                        t0 = b * NT + q * TPC
                        sp.dma_start(out_t[b, :, q * TPC:(q + 1) * TPC, :], xn[:, t0:t0 + TPC, :]).then_inc(s_out, 16)
                sp.wait_ge(s_out, 16 * B * NC)

            @block.gpsimd
            def _(pool):
                nc.gpsimd.memset(ident[:, :], 0.0).then_inc(s_const, 1)
                pool.wait_ge(s_const, 1)
                nc.gpsimd.affine_select(out=ident[:, :], in_=ident[:, :], compare_op=ALU.not_equal, fill=1.0,
                                        base=0, pattern=[[-1, P]], channel_multiplier=1).then_inc(s_const, 1)
                nc.gpsimd.memset(ones[:, :], 1.0).then_inc(s_const, 1)
                nc.gpsimd.iota(steps_ii, pattern=[[1, CHUNK + 1]], base=0, channel_multiplier=0).then_inc(s_iota, 1)
                pool.wait_ge(s_iota, 1)
                nc.gpsimd.tensor_copy(steps, steps_ii).then_inc(s_steps, 1)
                nc.gpsimd.memset(headmask[:, :], 0.0)
                nc.gpsimd.memset(U[:, :, :, :], 0.0)
                nc.gpsimd.memset(vec[:, :, :, :], 0.0)
                nc.gpsimd.memset(w_sb[:, :, :], 0.0).then_inc(s_const, 1)
                pool.wait_ge(s_const, 4)
                nc.gpsimd.memset(headmask[:, 0:HG], 1.0).then_inc(s_const, 1)
                pool.wait_ge(s_const, 5)
                nc.gpsimd.affine_select(out=headmask[:, 0:HG], in_=headmask[:, 0:HG], compare_op=ALU.is_ge, fill=0.0,
                                        base=0, pattern=[[-E, HG]], channel_multiplier=1).then_inc(s_const, 1)
                pool.wait_ge(s_const, 6)
                nc.gpsimd.affine_select(out=headmask[:, 0:HG], in_=headmask[:, 0:HG], compare_op=ALU.is_gt, fill=0.0,
                                        base=E, pattern=[[E, HG]], channel_multiplier=-1).then_inc(s_const, 1)

                def fill(b):
                    if b == 0:
                        pool.wait_ge(s_condT, 1)
                    else:
                        pool.wait_ge(s_pp, b)
                    nc.gpsimd.memset(prob, NEG).then_inc(s_neg, 1)

                def add_rows(b):
                    pool.wait_ge(s_orow, b + 1)
                    for t in range(NT):
                        if b == 0 or t % 2 == 0:
                            nc.gpsimd.tensor_tensor(xn[:, b * NT + t, :], xn[:, b * NT + t, :], orow,
                                                    ALU.add).then_inc(s_add, 1)

                def unit_spikes(b, c):
                    for g in range(G):
                        u = (b * NC + c) * G + g
                        pool.wait_ge(s_xT, u + 1)
                        pool.wait_ge(s_spk, u + 1)
                        xs = xT[:, chunk_slot(b, c), g, :]
                        nc.gpsimd.tensor_tensor(xs, xs, spikes[:, u % 2, :], ALU.add).then_inc(s_x1T, 1)

                fill(0)
                for c in range(NC):
                    unit_spikes(0, c)
                for c in range(NC - 1):
                    unit_spikes(1, c)
                    if c == 1:
                        fill(1)
                    if c == 2:
                        add_rows(0)
                unit_spikes(1, NC - 1)
                add_rows(1)

            @block.scalar
            def _(act):
                def bank_evict(use, dst):
                    act.wait_ge(s_bk, use + 1)
                    nc.scalar.copy(dst, pbk[use % 2][:, :]).then_inc(s_bkout, 1)

                def weight_evict(dst, use):
                    for k in range(G):
                        bank_evict(use + k, dst[:, k, :])

                def unit_evict(b, c):
                    for g in range(G):
                        u = (b * NC + c) * G + g
                        act.wait_ge(s_pin, u + 1)
                        if u >= G:
                            act.wait_ge(s_spk, u - G + 1)
                        nc.scalar.activation(rate2[:, g, :].rearrange("p (n two) -> p n two", two=2),
                                             pin[u % 2][:, :].unsqueeze(2).to_broadcast([P, CHUNK, 2]),
                                             ACT.Relu, scale=DT).then_inc(s_rate, 1)
                        if g == 0 and b * NC + c == SLOTS:
                            act.wait_ge(s_sp, 1)
                        if g == 0 and b * NC + c == SLOTS - 2:
                            act.wait_ge(s_tp, 1)
                        nc.scalar.copy(xT[:, chunk_slot(b, c), g, :], pin[u % 2][:, :]).then_inc(s_xT, 1)

                def back_evict(b, c):
                    for t in range(TPC):
                        bank_evict(use_back(b * NC + c) + t, xn[:, b * NT + c * TPC + t, :])

                def A_evict(b, c):
                    n = b * NC + c
                    act.wait_ge(s_Ar, n + 1)
                    nc.scalar.copy(A_rows[:, :], pAP[:, 0:P]).then_inc(s_Are, 1)
                    act.wait_ge(s_Ap, n + 1)
                    if n >= 2:
                        act.wait_ge(s_Yc, n - 1)
                    nc.scalar.copy(A_sb[:, n % 2, :, :], pAP[:, P:2 * P].rearrange("p (t h) -> p t h", t=TPC)
                                   ).then_inc(s_A, 1)

                def by_group(x):
                    return x.rearrange("p k (j h) -> p k j h", j=G)

                def mid_y(b):
                    act.wait_ge(s_Yc, NC * (b + 1))
                    nc.scalar.copy(rows[:, :], pY[:, :]).then_inc(s_Ye, 1)
                    act.wait_ge(s_yc, b + 1)
                    nc.scalar.copy(vec[:, :, :, 0:HG], by_group(ps_comb[:, :, 0:H])).then_inc(s_y, 1)
                    act.wait_ge(s_qp, b + 1)
                    nc.scalar.copy(he_rows[:, :], ps_rows).then_inc(s_qe, 1)

                def mid_w(b):
                    act.wait_ge(s_wp, b + 1)
                    nc.scalar.mul(rows[:, :], pY[:, :], SCALE).then_inc(s_wr, 1)
                    act.wait_ge(s_wtr, b + 1)
                    nc.scalar.copy(by_group(w_sb[:, :, 0:H]), pS[:, :].rearrange(
                        "p (k j h) -> p k j h", k=G, j=G)[:, :, :, 0:HG]).then_inc(s_w, 1)

                def mid_exp(b):
                    act.wait_ge(s_mx, b + 1)
                    nc.scalar.activation(prob, prob, ACT.Exp, bias=nmx[:, :],
                                         accum_out=psum_rows[:, :]).then_inc(s_ex, 1)
                    act.wait_ge(s_pp, b + 1)
                    nc.scalar.copy(pT[:, :, :], pY[:, :].rearrange("p (t n) -> p t n", t=TPC)).then_inc(s_pT, 1)

                def mid_part(b):
                    act.wait_ge(s_mb, b + 1)
                    nc.scalar.activation(part[:, :], ps_mcol, ACT.Exp, bias=mx[:, :], scale=-1.0).then_inc(s_f, 1)

                def mid_z(b):
                    act.wait_ge(s_zp, b + 1)
                    nc.scalar.copy(rows[:, :], pS[:, :]).then_inc(s_ze, 1)
                    act.wait_ge(s_zc, b + 1)
                    nc.scalar.copy(vec[:, :, :, 0:HG], by_group(ps_comb[:, :, 0:H])).then_inc(s_z, 1)
                    act.wait_ge(s_op, b + 1)
                    nc.scalar.copy(he_rows[:, :], ps_rows).then_inc(s_oe, 1)

                def mid_row(b):
                    act.wait_ge(s_yp, b + 1)
                    if b:
                        act.wait_ge(s_add, NT)
                    nc.scalar.copy(orow, pS[:, :]).then_inc(s_orow, 1)

                act.wait_ge(s_condT, 1)
                cols = pM[:, 0:B * G].rearrange("p (b g) -> p b g", b=B)
                nc.scalar.copy(vinit[:, :, :], cols).then_inc(s_vinit, 1)
                nc.scalar.copy(tcol[:, :, :], cols.rearrange("p b g -> p g b")).then_inc(s_tcol, 1)
                unit_evict(0, 0)
                weight_evict(wtT, USE_WT)
                weight_evict(wqT, USE_WQ)
                unit_evict(0, 1)
                weight_evict(wvT, USE_WV)
                A_evict(0, 0)
                back_evict(0, 0)
                act.wait_ge(s_xor, 1)
                nc.scalar.activation(masks_f, masks, ACT.Square, accum_out=xorsum[:, :]).then_inc(s_xs, 1)
                unit_evict(0, 2)
                weight_evict(woT, USE_WO)
                A_evict(0, 1)
                back_evict(0, 1)
                unit_evict(0, 3)
                A_evict(0, 2)
                back_evict(0, 2)
                unit_evict(1, 0)
                A_evict(0, 3)
                back_evict(0, 3)
                mid_y(0)
                mid_w(0)
                unit_evict(1, 1)
                mid_exp(0)
                mid_part(0)
                mid_z(0)
                unit_evict(1, 2)
                mid_row(0)
                A_evict(1, 0)
                back_evict(1, 0)
                A_evict(1, 1)
                back_evict(1, 1)
                unit_evict(1, 3)
                A_evict(1, 2)
                back_evict(1, 2)
                A_evict(1, 3)
                back_evict(1, 3)
                mid_y(1)
                mid_w(1)
                mid_exp(1)
                mid_part(1)
                mid_z(1)
                mid_row(1)

            @block.vector
            def _(dve):
                n = [0]

                def link(ins):
                    n[0] += 1
                    ins.then_inc(s_dve, 1)
                    dve.wait_ge(s_dve, n[0])

                def mark(ins):
                    n[0] += 1
                    ins.then_inc(s_dve, 1)

                def catch_up():
                    dve.wait_ge(s_dve, n[0])

                def pair(b, c, pr, mid=()):
                    k = b * NC + c
                    gs = (2 * pr, 2 * pr + 1)
                    start = vinit[:, b, 2 * pr:2 * pr + 2] if c == 0 else vend[:, k - 1, 2 * pr:2 * pr + 2]
                    if c == 0 and pr == 0:
                        dve.wait_ge(s_vinit, 1)
                    link(nc.vector.tensor_copy(path[:, 2 * pr:2 * pr + 2, 1], start))
                    for g in gs:
                        dve.wait_ge(s_rate, k * G + g + 1)
                        mark(nc.vector.tensor_tensor_scan(path[:, g, 2:PATH], rate2[:, g, :], rate2[:, g, :],
                                                          path[:, g, 1:2], ALU.add, ALU.add))
                    if len(mid) > 0:
                        mid[0](0)
                    catch_up()
                    for i, g in enumerate(gs):
                        mark(nc.vector.tensor_scalar(late[:, i, 0:CHUNK], path[:, g, 3:PATH:2], 1.0, 0.0, ALU.is_lt,
                                                     ALU.add, accum_out=cnt[:, i:i + 1]))
                        catch_up()
                    for i, g in enumerate(gs):
                        mark(nc.vector.scalar_tensor_tensor(late[:, i, 0:CHUNK], steps[:, 0:CHUNK], cnt[:, i:i + 1],
                                                            rate2[:, g, 0:2 * CHUNK:2], ALU.is_equal, ALU.mult,
                                                            accum_out=rstar[:, k, g:g + 1]))
                        catch_up()
                        mark(nc.vector.scalar_tensor_tensor(late[:, i, 0:CHUNK + 1], steps, cnt[:, i:i + 1],
                                                            path[:, g, 1:PATH:2], ALU.is_equal, ALU.mult,
                                                            accum_out=vprev[:, i:i + 1]))
                        catch_up()
                        mark(nc.vector.scalar_tensor_tensor(
                            late[:, i, :].rearrange("p (n two) -> p n two", two=2),
                            path[:, g, 1:PATH - 2:2].unsqueeze(2).to_broadcast([P, CHUNK, 2]), 1.0,
                            rate2[:, g, :].rearrange("p (n two) -> p n two", two=2), ALU.is_ge, ALU.mult))
                    if len(mid) > 1:
                        mid[1](0)
                    catch_up()
                    rs = rstar[:, k, 2 * pr:2 * pr + 2]
                    link(nc.vector.tensor_tensor(vpre[:, :], vprev[:, :], rs, ALU.add))
                    for _ in range(SUB - 1):
                        link(nc.vector.scalar_tensor_tensor(nvlt[:, :], vpre[:, :], 1.0, vpre[:, :], ALU.is_ge,
                                                            ALU.subtract))
                        link(nc.vector.tensor_tensor(vpre[:, :], rs, nvlt[:, :], ALU.subtract))
                    mark(nc.vector.scalar_tensor_tensor(nvlt[:, :], vpre[:, :], 1.0, vpre[:, :], ALU.is_ge,
                                                        ALU.subtract))
                    mark(nc.vector.tensor_scalar(spk[:, :], vpre[:, :], 1.0, PER_SPIKE, ALU.is_ge, ALU.mult))
                    catch_up()
                    link(nc.vector.tensor_scalar(vstar[:, :], nvlt[:, :], -1.0, None, ALU.mult))
                    for i, g in enumerate(gs):
                        mark(nc.vector.tensor_tensor_scan(late[:, i, :], late[:, i, :], late[:, i, :],
                                                          vstar[:, i:i + 1], ALU.add, ALU.add))
                    catch_up()
                    mark(nc.vector.tensor_copy(vend[:, k, 2 * pr:2 * pr + 2], late[:, :, 2 * CHUNK - 1]))
                    for i, g in enumerate(gs):
                        u = k * G + g
                        if u >= 2:
                            dve.wait_ge(s_x1T, u - 1)
                        nc.vector.tensor_scalar(spikes[:, u % 2, :], steps[:, 0:CHUNK], cnt[:, i:i + 1],
                                                spk[:, i:i + 1], ALU.is_equal, ALU.mult).then_inc(s_spk, 1)
                    dve.wait_ge(s_spk, u + 1)
                    if len(mid) > 2:
                        mid[2](0)

                def time_vector():
                    dve.wait_ge(s_tp, 1)
                    dve.wait_ge(s_const, 7)
                    for b in range(B):
                        nc.vector.tensor_tensor(tpd[:, :, b, :],
                                                ps_tp[:, :, b].unsqueeze(2).to_broadcast([P, G, HG]), hm_b(),
                                                ALU.mult).then_inc(s_tpd, 1)
                    dve.wait_ge(s_Up, 1)
                    nc.vector.tensor_copy(U[:, :, :, 0:H], ps_U).then_inc(s_U, 1)

                def compare_masks():
                    dve.wait_ge(s_mask, 16)
                    dve.wait_ge(s_mrow, 16 * (1 + NC))
                    words = masks.rearrange("p (r w) -> p r w", r=NT)
                    nc.vector.tensor_tensor(words, words, row0.unsqueeze(1).to_broadcast([P, NT, SEQ // 4]),
                                            ALU.bitwise_xor).then_inc(s_xor, 1)

                def mid_q(b):
                    dve.wait_ge(s_qt, b + 1)
                    nc.vector.tensor_tensor(qsel[:, :, :], ps_cols, hm_slab(), ALU.mult).then_inc(s_q, 1)

                def mid_scores(b):
                    dve.wait_ge(s_neg, b + 1)
                    dve.wait_ge(s_sp, b + 1)
                    nc.vector.copy_predicated(prob, mask0, pS[:, :]).then_inc(s_sc, 1)
                    dve.wait_ge(s_sc, b + 1)
                    link(nc.vector.reduce_max(mx[:, :], prob, AX))
                    nc.vector.tensor_scalar(nmx[:, :], mx[:, :], -1.0, None, ALU.mult).then_inc(s_mx, 1)

                def mid_max(b):
                    dve.wait_ge(s_mt, b + 1)
                    link(nc.vector.reduce_max(mrow, ps_mrow.rearrange("o (c h) -> o h c", c=G), AX))
                    nc.vector.tensor_copy(mrow_all, mrow.unsqueeze(1).to_broadcast([1, G, SLAB])
                                          ).then_inc(s_mr, 1)

                def mid_share(b):
                    dve.wait_ge(s_f, b + 1)
                    nc.vector.tensor_tensor(share[:, :], part[:, :], psum_rows[:, :], ALU.mult).then_inc(s_sh, 1)

                def mid_comb(b):
                    dve.wait_ge(s_tot, b + 1)
                    link(nc.vector.reciprocal(rtot[:, :], ps_tot))
                    nc.vector.tensor_scalar(comb[:, :], same[:, :], part[:, :], rtot[:, :], ALU.mult,
                                            ALU.mult).then_inc(s_cb, 1)

                def mid_o(b):
                    dve.wait_ge(s_ot, b + 1)
                    link(nc.vector.tensor_tensor(osel[:, :, :], ps_cols, hm_slab(), ALU.mult))
                    nc.vector.reduce_sum(ocol[:, :], osel[:, :, :], AX).then_inc(s_o, 1)

                dve.wait_ge(s_const, 3)
                nc.vector.reduce_sum(same[:, :], ident[:, :].rearrange("p (i h) -> p h i", i=G), AX).then_inc(s_same, 1)
                dve.wait_ge(s_same, 1)
                nc.vector.tensor_copy(same_all[:, :, :], same[:, :].unsqueeze(1).to_broadcast([P, G, SLAB])
                                      ).then_inc(s_same, 1)
                dve.wait_ge(s_steps, 1)
                mids = {(1, 0, 1): (mid_q,), (1, 1, 0): (mid_scores, mid_max, mid_share),
                        (1, 1, 1): (mid_comb, mid_o)}
                for b in range(B):
                    for c in range(NC):
                        for pr in range(G // 2):
                            pair(b, c, pr, mids.get((b, c, pr), ()))
                            if (b, c, pr) == (0, 0, 0):
                                time_vector()
                            if (b, c, pr) == (0, 1, 0):
                                compare_masks()
                link(nc.vector.tensor_scalar(late[:, 0, 0:B * G], vinit[:, :, :].rearrange("p b g -> p (b g)"), 1.0,
                                             None, ALU.is_lt))
                link(nc.vector.tensor_reduce(good[:, 0:1], late[:, 0, 0:B * G], AX, ALU.min))
                link(nc.vector.tensor_scalar(late[:, 0, 0:UNITS], rstar[:, :, :].rearrange("p k g -> p (k g)"), 1.0,
                                             None, ALU.is_lt))
                link(nc.vector.tensor_reduce(good[:, 1:2], late[:, 0, 0:UNITS], AX, ALU.min))
                link(nc.vector.tensor_scalar(late[:, 0, 0:UNITS], vend[:, :, :].rearrange("p k g -> p (k g)"), 1.0,
                                             None, ALU.is_lt))
                link(nc.vector.tensor_reduce(good[:, 2:3], late[:, 0, 0:UNITS], AX, ALU.min))
                link(nc.vector.tensor_reduce(goodall[:, :], good[:, :], AX, ALU.min))
                dve.wait_ge(s_xs, 1)
                nc.vector.scalar_tensor_tensor(goodall[:, :], xorsum[:, :], 0.0, goodall[:, :], ALU.is_equal,
                                               ALU.mult).then_inc(s_gd, 1)
                for mid in (mid_q, mid_scores, mid_max, mid_share, mid_comb, mid_o):
                    mid(1)
                dve.wait_ge(s_badp, 1)
                nc.vector.tensor_scalar(verdict[:, :], ps_bad, FORCE or P - 0.5, None,
                                        ALU.is_lt).then_inc(s_vd, 1)
                dve.wait_ge(s_orow, B)
                for t in range(1, NT, 2):
                    nc.vector.tensor_tensor(xn[:, NT + t, :], xn[:, NT + t, :], orow, ALU.add).then_inc(s_add2, 1)

            @block.tensor
            def _(pe):
                def bank_fill(use, src):
                    if use >= 2:
                        pe.wait_ge(s_bkout, use - 1)
                    return pe_transpose_tile(pbk[use % 2], src).then_inc(s_bk, 1)

                def weight(w, use):
                    for k in range(G):
                        bank_fill(use + k, [w[:, j, k * P:(k + 1) * P] for j in range(G)])

                def unit_in(b, c):
                    pe.wait_ge(s_xin[b * NC + c], 16)
                    for g in range(G):
                        u = (b * NC + c) * G + g
                        if u >= 2:
                            pe.wait_ge(s_xT, u - 1)
                        pe_transpose_tile(pin[u % 2], [xn[:, b * NT + c * TPC + t, g * P:(g + 1) * P]
                                                       for t in range(TPC)]).then_inc(s_pin, 1)

                def back(b, c):
                    k = b * NC + c
                    slot = chunk_slot(b, c)
                    pe.wait_ge(s_x1T, (k + 1) * G)
                    if k == 0:
                        pe.wait_ge(s_U, 1)
                    if k > 0:
                        pe.wait_ge(s_Are, k)
                    pe_A(b, slot).then_inc(s_Ar, 1)
                    bank_fill(use_back(k), [xT[:, slot, g, 0:P] for g in range(G)])
                    pe.wait_ge(s_Are, k + 1)
                    if k > 0:
                        pe.wait_ge(s_A, k)
                    nc.tensor.transpose(pAP[:, P:2 * P], A_rows[:, :], ident[:, :]).then_inc(s_Ap, 1)
                    for t in range(1, TPC):
                        bank_fill(use_back(k) + t, [xT[:, slot, g, t * P:(t + 1) * P] for g in range(G)])
                    pe.wait_ge(s_A, k + 1)
                    pe.wait_ge(s_bkout, use_back(k) + TPC)
                    if k == NC:
                        pe.wait_ge(s_pT, 1)
                    pe_Y(b, c, k % 2).then_inc(s_Yc, 1)

                def mid_y(b):
                    pe.wait_ge(s_Ye, b + 1)
                    pe.wait_ge(s_same, 2)
                    pe_combine(same[:, :]).then_inc(s_yc, 1)
                    pe.wait_ge(s_y, b + 1)
                    pe_heads(wqT).then_inc(s_qp, 1)
                    pe.wait_ge(s_qe, b + 1)
                    nc.tensor.transpose(pM[:, P:2 * P], he_rows[:, :], ident[:, :]).then_inc(s_qt, 1)

                def mid_w(b):
                    pe.wait_ge(s_q, b + 1)
                    pe.wait_ge(s_wk, 16)
                    pe_w().then_inc(s_wp, 1)
                    pe.wait_ge(s_wr, b + 1)
                    if b:
                        pe.wait_ge(s_orow, b)
                    pe_transpose_tile(pS, [rows[:, k * P:(k + 1) * P] for k in range(G)]).then_inc(s_wtr, 1)
                    pe.wait_ge(s_w, b + 1)
                    pe_scores(b).then_inc(s_sp, 1)

                def mid_exp(b):
                    pe.wait_ge(s_mx, b + 1)
                    nc.tensor.transpose(ps_mrow, mx[:, :], ident[:, :]).then_inc(s_mt, 1)
                    pe.wait_ge(s_ex, b + 1)
                    pe_transpose_tile(pY, [prob[:, t * P:(t + 1) * P] for t in range(TPC)]).then_inc(s_pp, 1)
                    pe.wait_ge(s_mr, b + 1)
                    nc.tensor.matmul(ps_mcol, mrow_all.rearrange("o c h -> o (c h)"), ident[0:1, 0:1],
                                     start=True, stop=True).then_inc(s_mb, 1)
                    pe.wait_ge(s_pT, b + 1)
                    pe_z(b).then_inc(s_zp, 1)
                    pe.wait_ge(s_sh, b + 1)
                    nc.tensor.matmul(ps_tot, same_all[:, :, :].rearrange("p c h -> p (c h)"), share[:, :],
                                     start=True, stop=True).then_inc(s_tot, 1)

                def mid_z(b):
                    pe.wait_ge(s_cb, b + 1)
                    pe.wait_ge(s_ze, b + 1)
                    pe_combine(comb[:, :]).then_inc(s_zc, 1)
                    pe.wait_ge(s_z, b + 1)
                    pe_heads(wvT).then_inc(s_op, 1)
                    pe.wait_ge(s_oe, b + 1)
                    nc.tensor.transpose(pM[:, P:2 * P], he_rows[:, :], ident[:, :]).then_inc(s_ot, 1)

                def mid_row(b):
                    pe.wait_ge(s_o, b + 1)
                    for j in range(G):
                        last = nc.tensor.matmul(pS[:, :], ocol[:, j:j + 1].to_broadcast([P, P]), woT[:, j, :],
                                                start=(j == 0), stop=(j == G - 1))
                    last.then_inc(s_yp, 1)

                pe.wait_ge(s_const, 7)
                pe.wait_ge(s_cond, 16)
                nc.tensor.transpose(pM[:, 0:B * G], cond_rows, ident[0:B * G, 0:B * G]).then_inc(s_condT, 1)
                unit_in(0, 0)
                pe.wait_ge(s_wt, 16)
                weight(wstage, USE_WT)
                pe.wait_ge(s_wq, 16)
                weight(wq_sb, USE_WQ)
                pe.wait_ge(s_bkout, USE_WT + G)
                pe.wait_ge(s_tcol, 1)
                for j in range(G):
                    for k in range(G):
                        last = nc.tensor.matmul(ps_tp[:, j, :], wtT[:, k, j * P:(j + 1) * P], tcol[:, k, :],
                                                start=(k == 0), stop=(k == G - 1))
                last.then_inc(s_tp, 1)
                pe.wait_ge(s_tpd, B)
                for k in range(G):
                    for j in range(G):
                        last = nc.tensor.matmul(ps_U[:, k, :, j * HG:(j + 1) * HG], wq_sb[:, j, k * P:(k + 1) * P],
                                                tpd[:, j, :, :], start=True, stop=True)
                last.then_inc(s_Up, 1)
                unit_in(0, 1)
                pe.wait_ge(s_wv, 16)
                weight(wstage, USE_WV)
                back(0, 0)
                unit_in(0, 2)
                pe.wait_ge(s_wo, 16)
                weight(wstage, USE_WO)
                back(0, 1)
                unit_in(0, 3)
                back(0, 2)
                unit_in(1, 0)
                back(0, 3)
                mid_y(0)
                mid_w(0)
                unit_in(1, 1)
                mid_exp(0)
                mid_z(0)
                unit_in(1, 2)
                mid_row(0)
                back(1, 0)
                back(1, 1)
                unit_in(1, 3)
                back(1, 2)
                back(1, 3)
                pe.wait_ge(s_gd, 1)
                nc.tensor.matmul(ps_bad, ones[:, :].to_broadcast([P, P]), goodall[:, :], start=True, stop=True).then_inc(s_badp, 1)
                mid_y(1)
                mid_w(1)
                mid_exp(1)
                mid_z(1)
                mid_row(1)

        sc = cut(SEQ, True)[0:H, :]
        sel = cut(H * P)[0:H, :]
        onehot = cut(P)[0:H, :]
        mrows = cut(SEQ // 4).bitcast(u8)
        S = cut(SEQ)
        ST = cut(SEQ)
        O = cut(D)
        OT = cut(D).rearrange("p (j n) -> p j n", j=G)
        res = cut(D)
        tile = cut(D).rearrange("p (g n) -> p g n", g=G)
        v, r, a, m, n0, f = [cut(G).rearrange("p (g n) -> p g n", g=G) for _ in range(6)]
        rowmax, nrowmax, rowsum, rrow = [cut(1) for _ in range(4)]
        gA = cut(TPC * H)
        gy = cut(G * H).rearrange("p (k h) -> p k h", k=G)
        gw = cut(G * H).rearrange("p (k h) -> p k h", k=G)
        gq = cut(G * HG).rearrange("p (j h) -> p j h", j=G)
        pscore = [pin[0], pin[1], pbk[0], pbk[1]]
        pturn = [pAP, pY, pS, pM]

        g_sel = sem("g_sel")
        g_ld = sem("g_ld")
        g_tp = sem("g_tp")
        g_ev = sem("g_ev")
        g_bt = sem("g_bt")
        g_btp = sem("g_btp")
        g_bev = sem("g_bev")
        g_A = sem("g_A")
        g_Ae = sem("g_Ae")
        g_Y = sem("g_Y")
        g_ye = sem("g_ye")
        g_q = sem("g_q")
        g_qe = sem("g_qe")
        g_w = sem("g_w")
        g_we = sem("g_we")
        g_s = sem("g_s")
        g_se = sem("g_se")
        g_v = sem("g_v")
        g_ve = sem("g_ve")
        g_mk = sem("g_mk")
        g_neg = sem("g_neg")
        g_oh = sem("g_oh")
        g_bc = sem("g_bc")
        g_cp = sem("g_cp")
        g_mx = sem("g_mx")
        g_ex = sem("g_ex")
        g_st = sem("g_st")
        g_ste = sem("g_ste")
        g_o = sem("g_o")
        g_O = sem("g_O")
        g_ot = sem("g_ot")
        g_ote = sem("g_ote")
        g_y = sem("g_y")
        g_res = sem("g_res")
        g_out = sem("g_out")
        g_dve = sem("g_dve")
        g_go = sem("g_go")
        g_sum = sem("g_sum")


        def pe_A_general(b, c):
            for t in range(TPC):
                for g in range(G):
                    last = nc.tensor.matmul(pAP[:, t * H:(t + 1) * H], xT[:, c, g, t * P:(t + 1) * P],
                                            U[:, g, b, 0:H], start=(g == 0), stop=(g == G - 1))
            return last

        def pe_Y_general(b, c):
            for t in range(TPC):
                for k in range(G):
                    last = nc.tensor.matmul(pY[:, k * H:(k + 1) * H], xn[:, b * NT + c * TPC + t, k * P:(k + 1) * P],
                                            gA[:, t * H:(t + 1) * H], start=(c == 0 and t == 0 and k == 0),
                                            stop=(c == NC - 1 and t == TPC - 1), skip_group_check=True)
            return last

        with nc.Block() as block:
            @block.sync
            def _(sp):
                bad = sp.value_load(verdict[0:1, 0:1])
                with sp.If(bad > 0):
                    sp.sem_inc(g_out, 16)
                    for b in range(B):
                        with sp.Fori(0, NT) as t:
                            sp.wait_ge(g_tp, t + (b * NT + 1))
                            sp.dma_start(tile, x_t[b, :, bass.ds(t, 1), :]
                                         .rearrange("p t (g n) -> p (t g) n", g=G)).then_inc(g_ld, 16)
                        with sp.Fori(0, NT) as t:
                            sp.wait_ge(g_res, t + (b * NT + 1))
                            sp.dma_start(mrows, mask[bass.ds(t * P, P), :]).then_inc(g_mk, 16)
                            sp.wait_ge(g_res, t + (b * NT + 2))
                            sp.dma_start(out_t[b, :, bass.ds(t, 1), :],
                                         res.unsqueeze(1)).then_inc(g_out, 16)
                    sp.wait_ge(g_out, 16 * (B * NT + 1))
                sp.end_ifs()

            @block.gpsimd
            def _(pool):
                bad = pool.value_load(verdict[0:1, 0:1])
                with pool.If(bad > 0):
                    nc.gpsimd.memset(sel, 1.0).then_inc(g_sel, 1)
                    pool.wait_ge(g_sel, 1)
                    nc.gpsimd.affine_select(out=sel, in_=sel, compare_op=ALU.is_ge, fill=0.0, base=0,
                                            pattern=[[1, H * P]], channel_multiplier=-P).then_inc(g_sel, 1)
                    pool.wait_ge(g_sel, 2)
                    nc.gpsimd.affine_select(out=sel, in_=sel, compare_op=ALU.is_gt, fill=0.0, base=P,
                                            pattern=[[-1, H * P]], channel_multiplier=P).then_inc(g_sel, 1)
                    with pool.Fori(0, B * NT * H) as i:
                        pool.wait_ge(g_st, i + 1)
                        pool.sem_inc(g_go, 1)
                        nc.gpsimd.memset(S, NEG).then_inc(g_neg, 1)
                pool.end_ifs()

            @block.scalar
            def _(act):
                bad = act.value_load(verdict[0:1, 0:1])
                with act.If(bad > 0):
                    act.sem_inc(g_ev, 1)
                    act.sem_inc(g_bev, 1)
                    for b in range(B):
                        with act.Fori(0, NC) as c:
                            with act.Fori(0, TPC) as t:
                                act.wait_ge(g_tp, c * TPC + t + (b * NT + 2))
                                nc.scalar.copy(xT[:, bass.ds(c, 1), :, bass.ds(t * P, P)],
                                               pin[0][:, :].rearrange("p (g n) -> p g n", g=G).unsqueeze(1)).then_inc(g_ev, 1)
                        with act.Fori(0, NT) as t:
                            act.wait_ge(g_btp, t + (b * NT + 2))
                            nc.scalar.copy(xn[:, bass.ds(t + b * NT, 1), :], pin[1][:, :].unsqueeze(1)).then_inc(g_bev, 1)
                        for c in range(NC):
                            k = b * NC + c
                            act.wait_ge(g_A, k + 1)
                            nc.scalar.copy(gA, pAP[:, 0:TPC * H]).then_inc(g_Ae, 1)
                        act.wait_ge(g_Y, NC * (b + 1))
                        nc.scalar.copy(gy, pY[:, 0:G * H].rearrange("p (k h) -> p k h", k=G)).then_inc(g_ye, 1)
                        act.wait_ge(g_w, b + 1)
                        nc.scalar.mul(gw, ps_w, SCALE).then_inc(g_we, 1)
                        for c in range(NC):
                            k = b * NC + c
                            act.wait_ge(g_s, k + 1)
                            nc.scalar.copy(sc[:, c * CHUNK:(c + 1) * CHUNK], pS[0:H, :]).then_inc(g_se, 1)
                        for t in range(NT):
                            i = b * NT + t
                            act.wait_ge(g_v, i + 1)
                            nc.scalar.copy(xT[:, t // TPC, :, (t % TPC) * P:(t % TPC + 1) * P],
                                           pbk[t % 2][:, :].rearrange("p (g n) -> p g n", g=G)).then_inc(g_ve, 1)
                        with act.Fori(0, NT) as t:
                            with act.Fori(0, H) as h:
                                i = t * H + h
                                act.wait_ge(g_mx, i + (b * NT * H + 1))
                                nc.scalar.activation(S, S, ACT.Exp, bias=nrowmax, accum_out=rowsum).then_inc(g_ex, 1)
                                act.wait_ge(g_st, i + (b * NT * H + 2))
                                for q in range(NC):
                                    nc.scalar.copy(ST[:, q * CHUNK:(q + 1) * CHUNK], pturn[q][:, :]).then_inc(g_ste, 1)
                            act.wait_ge(g_ot, t + (b * NT + 1))
                            nc.scalar.copy(OT, pin[1][:, :].rearrange("p (j n) -> p j n", j=G)).then_inc(g_ote, 1)
                act.end_ifs()

            @block.vector
            def _(dve):
                bad = dve.value_load(verdict[0:1, 0:1])
                with dve.If(bad > 0):
                    dve.sem_inc(g_res, 1)
                    dve.wait_ge(g_sel, 3)
                    OPS = 1 + SUB * 7 + 2
                    for b in range(B):
                        dve.wait_ge(g_ev, NT * (b + 1) + 1)
                        nc.vector.tensor_copy(v, vinit[:, b, :].unsqueeze(2)).then_inc(g_dve, 1)
                        with dve.Fori(0, NC) as c:
                            with dve.Fori(0, CHUNK) as s:
                                before = (c * CHUNK + s) * OPS + (b * (SEQ * OPS + 1) + 1)
                                done = [0]

                                def link(ins):
                                    ins.then_inc(g_dve, 1)
                                    done[0] += 1
                                    dve.wait_ge(g_dve, before + done[0])

                                xs = xT[:, bass.ds(c, 1), :, bass.ds(s, 1)].rearrange("p c g n -> p (c g) n")
                                dve.wait_ge(g_dve, before)
                                link(nc.vector.tensor_scalar(r, xs, 0.0, DT, ALU.max, ALU.mult))
                                for _ in range(SUB):
                                    link(nc.vector.tensor_tensor(a, v, r, ALU.add))
                                    link(nc.vector.tensor_scalar(m, a, TWO23, TWO23, ALU.min, ALU.add))
                                    link(nc.vector.tensor_scalar(n0, m, TWO23, None, ALU.subtract))
                                    link(nc.vector.tensor_tensor(f, n0, a, ALU.is_gt))
                                    link(nc.vector.tensor_tensor(n0, n0, f, ALU.subtract))
                                    link(nc.vector.tensor_tensor(v, a, n0, ALU.subtract))
                                    link(nc.vector.scalar_tensor_tensor(v, a, TWO23, v, ALU.is_lt, ALU.mult))
                                link(nc.vector.tensor_tensor(a, a, v, ALU.subtract))
                                link(nc.vector.scalar_tensor_tensor(xs, a, PER_SPIKE, xs, ALU.mult, ALU.add))
                                assert done[0] == OPS
                        dve.wait_ge(g_dve, (b + 1) * (SEQ * OPS + 1))
                        with dve.Fori(0, NC) as c:
                            with dve.Fori(0, TPC) as t:
                                dve.wait_ge(g_btp, c * TPC + t + (b * NT + 1))
                                nc.vector.tensor_copy(tile, xT[:, bass.ds(c, 1), :, bass.ds(t * P, P)]
                                                      .rearrange("p c g n -> p (c g) n")).then_inc(g_bt, 1)
                        dve.wait_ge(g_q, b + 1)
                        nc.vector.tensor_tensor(gq, ps_q, hm_b(), ALU.mult).then_inc(g_qe, 1)
                        with dve.Fori(0, NT) as t:
                            with dve.Fori(0, H) as h:
                                i = t * H + h
                                dve.wait_ge(g_mk, (t + (b * NT + 1)) * 16)
                                nc.vector.tensor_copy(onehot, sel[:, bass.ds(h * P, P)]).then_inc(g_oh, 1)
                                dve.wait_ge(g_neg, i + (b * NT * H + 1))
                                dve.wait_ge(g_bc, i + (b * NT * H + 1))
                                dve.sem_inc(g_go, 1)
                                for q in range(NC):
                                    cs = slice(q * CHUNK, (q + 1) * CHUNK)
                                    nc.vector.copy_predicated(S[:, cs], mrows[:, cs], pscore[q][:, :]).then_inc(g_cp, 1)
                                dve.wait_ge(g_cp, (i + (b * NT * H + 1)) * NC)
                                nc.vector.reduce_max(rowmax, S, AX).then_inc(g_sum, 1)
                                dve.wait_ge(g_sum, i * 2 + (b * NT * H * 2 + 1))
                                nc.vector.tensor_scalar(nrowmax, rowmax, -1.0, None, ALU.mult).then_inc(g_mx, 1)
                                dve.wait_ge(g_o, i + (b * NT * H + 1))
                                nc.vector.reciprocal(rrow, rowsum).then_inc(g_sum, 1)
                                dve.wait_ge(g_sum, i * 2 + (b * NT * H * 2 + 2))
                                nc.vector.tensor_scalar(O[:, bass.ds(h * E, E)], pin[0][:, 0:E], rrow, None,
                                                        ALU.mult).then_inc(g_O, 1)
                            dve.wait_ge(g_y, t + (b * NT + 1))
                            dve.wait_ge(g_out, (t + (b * NT + 1)) * 16)
                            nc.vector.tensor_tensor(res.unsqueeze(1), pbk[0][:, :].unsqueeze(1),
                                                    xn[:, bass.ds(t + b * NT, 1), :], ALU.add).then_inc(g_res, 1)
                dve.end_ifs()

            @block.tensor
            def _(pe):
                bad = pe.value_load(verdict[0:1, 0:1])
                with pe.If(bad > 0):
                    pe.sem_inc(g_tp, 1)
                    pe.sem_inc(g_btp, 1)
                    pe.sem_inc(g_st, 1)
                    for b in range(B):
                        with pe.Fori(0, NT) as t:
                            pe.wait_ge(g_ld, (t + (b * NT + 1)) * 16)
                            pe.wait_ge(g_ev, t + (b * NT + 1))
                            pe_transpose_tile(pin[0], [tile[:, g, :] for g in range(G)]).then_inc(g_tp, 1)
                        with pe.Fori(0, NT) as t:
                            pe.wait_ge(g_bt, t + (b * NT + 1))
                            pe.wait_ge(g_bev, t + (b * NT + 1))
                            pe_transpose_tile(pin[1], [tile[:, g, :] for g in range(G)]).then_inc(g_btp, 1)
                        pe.wait_ge(g_bev, NT * (b + 1) + 1)
                        for c in range(NC):
                            k = b * NC + c
                            pe_A_general(b, c).then_inc(g_A, 1)
                            pe.wait_ge(g_Ae, k + 1)
                            pe_Y_general(b, c).then_inc(g_Y, 1)
                        pe.wait_ge(g_ye, b + 1)
                        for j in range(G):
                            for k in range(G):
                                last = nc.tensor.matmul(ps_q[:, j, :], wqT[:, k, j * P:(j + 1) * P],
                                                        gy[:, k, j * HG:(j + 1) * HG], start=(k == 0), stop=(k == G - 1))
                        last.then_inc(g_q, 1)
                        pe.wait_ge(g_qe, b + 1)
                        for k in range(G):
                            for j in range(G):
                                last = nc.tensor.matmul(ps_w[:, k, j * HG:(j + 1) * HG],
                                                        wk_sb[:, j, k * P:(k + 1) * P], gq[:, j, :],
                                                        start=True, stop=True)
                        last.then_inc(g_w, 1)
                        pe.wait_ge(g_we, b + 1)
                        for c in range(NC):
                            if b * NC + c:
                                pe.wait_ge(g_se, b * NC + c)
                            for k in range(G):
                                last = nc.tensor.matmul(pS[0:H, :], gw[:, k, :], xT[:, c, k, :],
                                                        start=(k == 0), stop=(k == G - 1))
                            last.then_inc(g_s, 1)
                        for t in range(NT):
                            i = b * NT + t
                            if i >= 2:
                                pe.wait_ge(g_ve, i - 1)
                            for g in range(G):
                                last = nc.tensor.matmul(pbk[t % 2][:, :],
                                                        xT[:, t // TPC, g, (t % TPC) * P:(t % TPC + 1) * P],
                                                        wvT[:, g, :], start=(g == 0), stop=(g == G - 1))
                            last.then_inc(g_v, 1)
                        pe.wait_ge(g_ve, NT * (b + 1))
                        pe.wait_ge(g_se, NC * (b + 1))
                        with pe.Fori(0, NT) as t:
                            with pe.Fori(0, G) as hg:
                                with pe.Fori(0, HG) as hh:
                                    i = t * H + hg * HG + hh
                                    pe.wait_ge(g_oh, i + (b * NT * H + 1))
                                    for q in range(NC):
                                        last = nc.tensor.matmul(pscore[q][:, :], onehot,
                                                                sc[:, q * CHUNK:(q + 1) * CHUNK], start=True, stop=True)
                                    last.then_inc(g_bc, 1)
                                    pe.wait_ge(g_ex, i + (b * NT * H + 1))
                                    for q in range(NC):
                                        last = pe_transpose_tile(pturn[q], [S[:, (q * TPC + n) * P:(q * TPC + n + 1) * P]
                                                                            for n in range(TPC)])
                                    last.then_inc(g_st, 1)
                                    pe.wait_ge(g_ste, (i + (b * NT * H + 1)) * NC)
                                    for n in range(NT):
                                        vh = xT[:, n // TPC, bass.ds(hg, 1), bass.ds(hh * E + (n % TPC) * P, E)]
                                        last = nc.tensor.matmul(pin[0][:, 0:E], ST[:, n * P:(n + 1) * P],
                                                                vh.rearrange("p g n -> p (g n)"),
                                                                start=(n == 0), stop=(n == NT - 1))
                                    last.then_inc(g_o, 1)
                            pe.wait_ge(g_O, (t + (b * NT + 1)) * H)
                            pe_transpose_tile(pin[1], [O[:, j * P:(j + 1) * P] for j in range(G)]).then_inc(g_ot, 1)
                            pe.wait_ge(g_ote, t + (b * NT + 1))
                            for j in range(G):
                                last = nc.tensor.matmul(pbk[0][:, :], OT[:, j, :], woT[:, j, :], start=(j == 0),
                                                        stop=(j == G - 1))
                            last.then_inc(g_y, 1)
                pe.end_ifs()


_INS = ['x', 'cond_1024', 'mask_SxS_bk0', 'L1_cond_Wq', 'L1_cond_Wk', 'L1_cond_Wv', 'L1_cond_Wt', 'L1_cond_Wo']
_OUTS = [((2, 2048, 512), 'float32')]


def kernel(**inputs):
    import numpy as _np
    import concourse.bacc as _bacc
    from concourse import mybir as _mybir
    from concourse.bass_utils import run_bass_kernel_spmd as _run

    nc = _bacc.Bacc("TRN2", target_bir_lowering=False, num_devices=1)
    arrays, args = {}, []
    for name in _INS:
        a = _np.ascontiguousarray(inputs[name])
        arrays[f"in_{name}_dram"] = a
        args.append(nc.dram_tensor(f"in_{name}_dram", a.shape, _mybir.dt.from_np(a.dtype), kind="ExternalInput").ap())
    for i, (shape, dtype) in enumerate(_OUTS):
        dt = _mybir.dt.from_np(_np.dtype(dtype))
        args.append(nc.dram_tensor(f"out_{i}_dram", shape, dt, kind="ExternalOutput").ap())
    spiking_residual_attention(nc, *args)
    r = _run(nc, [arrays], core_ids=[0])
    got = tuple(r.results[0][f"out_{i}_dram"] for i in range(len(_OUTS)))
    return got[0]
```

```python
import concourse.bass as bass
from concourse import mybir
from contextlib import ExitStack


def spiking_residual_attention(nc, x, cond, mask, wq, wk, wv, wt, wo, out, FORCE=None):
    fp32 = mybir.dt.float32
    i32 = mybir.dt.int32
    u8 = mybir.dt.uint8
    ALU = mybir.AluOpType
    ACT = mybir.ActivationFunctionType
    AX = mybir.AxisListType.X

    B, SEQ, D = x.shape
    H = 16
    E = D // H
    P = 128
    G = D // P
    SUB = 4
    CHUNK = 512
    NC = SEQ // CHUNK
    TPC = CHUNK // P
    NT = SEQ // P
    HG = P // E
    SLAB = 32
    SLOTS = NC + 2
    DT = 0.001
    PER_SPIKE = 999.99993896484375
    SCALE = float(E) ** -0.5
    NEG = -3.4028234663852886e38
    ARENA = 12980
    POOL_V = 2
    POOL_LAST = 1
    TWO23 = 8388608.0

    x_t = x.rearrange("b (t p) d -> b p t d", p=P)
    out_t = out.rearrange("b (t p) d -> b p t d", p=P)
    mask_words = mask.rearrange("(p r) s -> p (r s)", p=P).bitcast(i32)
    row0_words = mask[0:1, :].bitcast(i32)

    def w_rows(w):
        return w.rearrange("(j p) d -> p j d", p=P)

    ctx = ExitStack()
    with ctx:
        def sb(name, shape, dt=fp32):
            return ctx.enter_context(nc.sbuf_tensor(name, shape, dt))

        def pb(name):
            return ctx.enter_context(nc.psum_tensor(name, [P, 512], fp32))

        def sem(name):
            return ctx.enter_context(nc.semaphore(name))

        xn = sb("xn", [P, B * NT, D])
        xT = sb("xT", [P, SLOTS, G, CHUNK])
        wk_sb = sb("wk_sb", [P, G, D])
        wqT = sb("wqT", [P, G, D])
        wvT = sb("wvT", [P, G, D])
        woT = sb("woT", [P, G, D])
        ident = sb("ident", [P, P])
        ones = sb("ones", [P, 1])
        headmask = sb("headmask", [P, SLAB])
        same = sb("same", [P, SLAB])
        same_all = sb("same_all", [P, G, SLAB])
        U = sb("U", [P, G, B, SLAB])
        tcol = sb("tcol", [P, G, B])
        tpd = sb("tpd", [P, G, B, HG])
        A_rows = sb("A_rows", [P, P])
        A_sb = sb("A_sb", [P, 2, TPC, SLAB])
        rows = sb("rows", [P, D])
        he_rows = sb("he_rows", [P, P])
        vec = sb("vec", [P, G, G, SLAB])
        qsel = sb("qsel", [P, G, SLAB])
        w_sb = sb("w_sb", [P, G, SLAB])
        pT = sb("pT", [P, TPC, P])
        mx = sb("mx", [P, 1])
        nmx = sb("nmx", [P, 1])
        mrow = rows[0:1, P:P + SLAB]
        mrow_all = rows[0:1, 0:P].rearrange("o (c h) -> o c h", c=G)
        part = sb("part", [P, 1])
        psum_rows = sb("psum_rows", [P, 1])
        share = sb("share", [P, 1])
        rtot = sb("rtot", [P, 1])
        comb = sb("comb", [P, SLAB])
        osel = sb("osel", [P, G, SLAB])
        ocol = sb("ocol", [P, G])
        vinit = sb("vinit", [P, B, G])
        rstar = sb("rstar", [P, B * NC, G])
        vend = sb("vend", [P, B * NC, G])
        cnt = sb("cnt", [P, 2, G])
        vprev = sb("vprev", [P, G])
        vpre = sb("vpre", [P, G])
        nvlt = sb("nvlt", [P, G])
        vstar = sb("vstar", [P, G])
        spk = sb("spk", [P, G])
        good = sb("good", [P, 4])
        goodall = sb("goodall", [P, 1])
        xorsum = sb("xorsum", [P, NC])
        verdict = sb("verdict", [P, 1], i32)
        all_bits = sb("all_bits", [P, 1], i32)
        arena = sb("arena", [P, ARENA])
        at = [0]

        def cut(n, fresh=False):
            if fresh:
                at[0] = 0
            at[0] += n
            assert at[0] <= ARENA
            return arena[:, at[0] - n:at[0]]

        rate2 = cut(G * 2 * CHUNK, True).rearrange("p (g n) -> p g n", g=G)
        PATH = 2 * CHUNK + 2
        path = cut(G * PATH).rearrange("p (g n) -> p g n", g=G)
        late = path[:, :, 0:2 * CHUNK]
        left = cut(CHUNK + 2)
        spikes = cut(G * (CHUNK + 2)).rearrange("p (g n) -> p g n", g=G)
        picked = cut(CHUNK + 1)
        row_parts = picked[:, 0:D]
        junk = cut(CHUNK + 1)
        prob = cut(CHUNK)
        cond_rows = prob[0:B * G, 0:P]
        orow = cut(D)
        row0 = orow.bitcast(i32)
        left_ii = late[:, 0, 0:CHUNK + 2].bitcast(i32)
        mask0 = cut(CHUNK // 4).bitcast(u8)
        wq_sb = xT[:, SLOTS - 1, :, :]
        wstage = xT[:, SLOTS - 2, :, :]
        wtT = xT[:, SLOTS - 3, :, :]
        masks = xn[:, NT:2 * NT, :].rearrange("p t d -> p (t d)").bitcast(i32)
        masks_f = xn[:, NT:2 * NT, :].rearrange("p t d -> p (t d)")

        pin = [pb("pin0"), pb("pin1")]
        pbk = [pb("pbk0"), pb("pbk1")]
        pAP = pb("pAP")
        pY = pb("pY")
        pS = pb("pS")
        pM = pb("pM")
        ps_tp = pM[:, 0:8].rearrange("p (j b) -> p j b", b=B)
        ps_U = pM[:, 8:136].rearrange("p (k b h) -> p k b h", k=G, b=B)
        ps_q = pM[:, 136:152].rearrange("p (j h) -> p j h", j=G)
        ps_w = pM[:, 152:216].rearrange("p (k h) -> p k h", k=G)
        ps_rows = pM[:, 0:P]
        ps_cols = pM[:, P:2 * P].rearrange("p (j h) -> p j h", j=G)
        ps_comb = pM[:, 256:384].rearrange("p (k h) -> p k h", k=G)
        ps_mrow = pM[0:1, 384:512]
        ps_mcol = pAP[:, 384:385]
        ps_tot = pM[:, 0:1]
        ps_bad = pAP[:, 386:387]

        def pool_v(k):
            return POOL_V if k < B * NC - 1 else 0

        def chunk_slot(b, c):
            return (b * NC + c) % SLOTS

        USE_WT, USE_WQ, USE_WV, USE_WO = 0, G, 2 * G, 3 * G + TPC

        def use_back(k):
            return 3 * G if k == 0 else 4 * G + k * TPC

        def hm_b():
            return headmask[:, 0:HG].unsqueeze(1).to_broadcast([P, G, HG])

        def hm_slab():
            return headmask[:, :].unsqueeze(1).to_broadcast([P, G, SLAB])

        def pe_transpose_tile(dst, src):
            for i, s in enumerate(src):
                last = nc.tensor.transpose(dst[:, i * P:(i + 1) * P], s, ident[:, :])
            return last

        def slab(i):
            return slice(i * SLAB, (i + 1) * SLAB)

        def pe_A(b, slot):
            for g in range(G):
                for t in range(TPC):
                    last = nc.tensor.matmul(pAP[slab(t), 0:P], U[:, g, b, :], xT[:, slot, g, t * P:(t + 1) * P],
                                            start=(g == 0), stop=(g == G - 1))
            return last

        def pe_Y(b, c, par):
            for t in range(TPC):
                last = nc.tensor.matmul(pY[slab(t), :], A_sb[:, par, t, :], xn[:, b * NT + c * TPC + t, :],
                                        start=(c == 0), stop=(c == NC - 1), skip_group_check=True)
            return last

        def pe_combine(by):
            for k in range(G):
                last = nc.tensor.matmul(ps_comb[:, k, :], rows[:, k * P:(k + 1) * P], by, start=True, stop=True)
            return last

        def pe_heads(wT):
            for k in range(G):
                for j in range(G):
                    last = nc.tensor.matmul(ps_rows[slab(j), :], vec[:, k, j, :], wT[:, k, j * P:(j + 1) * P],
                                            start=(k == 0), stop=(k == G - 1))
            return last

        def pe_w():
            for j in range(G):
                last = nc.tensor.matmul(pY[slab(j), :], qsel[:, j, :], wk_sb[:, j, :], start=True, stop=True)
            return last

        def pe_scores(b):
            for g in range(G):
                for c in range(NC):
                    last = nc.tensor.matmul(pS[slab(c), :], w_sb[:, g, :], xT[:, chunk_slot(b, c), g, :],
                                            start=(g == 0), stop=(g == G - 1))
            return last

        def pe_z(b):
            for t in range(TPC):
                for c in range(NC):
                    last = nc.tensor.matmul(pS[slab(c), :], pT[:, t, slab(c)], xn[:, b * NT + c * TPC + t, :],
                                            start=(t == 0), stop=(t == TPC - 1))
            return last

        s_const = sem("s_const")
        s_iota = sem("s_iota")
        s_steps = sem("s_steps")
        s_cond = sem("s_cond")
        s_condT = sem("s_condT")
        s_vinit = sem("s_vinit")
        s_tcol = sem("s_tcol")
        s_xin = [sem(f"s_xin{i}") for i in range(B * NC)]
        s_xfirst = [sem(f"s_xfirst{g}") for g in range(G)]
        s_wt = sem("s_wt")
        s_wq = sem("s_wq")
        s_wk = sem("s_wk")
        s_wv = sem("s_wv")
        s_wo = sem("s_wo")
        s_mask = [sem(f"s_mask{q}") for q in range(NC)]
        s_row0 = sem("s_row0")
        s_mrow = sem("s_mrow")
        s_out = sem("s_out")
        s_pin = sem("s_pin")
        s_rate = sem("s_rate")
        s_xT = sem("s_xT")
        s_tp = sem("s_tp")
        s_tpd = sem("s_tpd")
        s_Up = sem("s_Up")
        s_U = sem("s_U")
        s_x1T = sem("s_x1T")
        s_bk = sem("s_bk")
        s_bkout = sem("s_bkout")
        s_Ar = sem("s_Ar")
        s_Are = sem("s_Are")
        s_Ap = sem("s_Ap")
        s_A = sem("s_A")
        s_Yc = sem("s_Yc")
        s_Ye = sem("s_Ye")
        s_yc = sem("s_yc")
        s_y = sem("s_y")
        s_qp = sem("s_qp")
        s_qe = sem("s_qe")
        s_qt = sem("s_qt")
        s_q = sem("s_q")
        s_wp = sem("s_wp")
        s_wr = sem("s_wr")
        s_wtr = sem("s_wtr")
        s_w = sem("s_w")
        s_neg = sem("s_neg")
        s_sp = sem("s_sp")
        s_sc = sem("s_sc")
        s_mx = sem("s_mx")
        s_mt = sem("s_mt")
        s_mr = sem("s_mr")
        s_mb = sem("s_mb")
        s_f = sem("s_f")
        s_sh = sem("s_sh")
        s_tot = sem("s_tot")
        s_cb = sem("s_cb")
        s_ex = sem("s_ex")
        s_pp = sem("s_pp")
        s_pT = sem("s_pT")
        s_zp = sem("s_zp")
        s_ze = sem("s_ze")
        s_zc = sem("s_zc")
        s_z = sem("s_z")
        s_op = sem("s_op")
        s_oe = sem("s_oe")
        s_ot = sem("s_ot")
        s_o = sem("s_o")
        s_same = sem("s_same")
        s_path = sem("s_path")
        s_cnt = sem("s_cnt")
        s_pick = sem("s_pick")
        s_vpre = sem("s_vpre")
        s_hot = sem("s_hot")
        s_rs = sem("s_rs")
        s_rst = sem("s_rst")
        s_late = sem("s_late")
        s_spk = sem("s_spk")
        s_height = sem("s_height")
        s_x1L = sem("s_x1L")
        s_ypp = sem("s_ypp")
        s_ype = sem("s_ype")
        s_yp = sem("s_yp")
        s_orow = sem("s_orow")
        s_add = sem("s_add")
        s_add2 = sem("s_add2")
        s_bits = sem("s_bits")
        s_inv = sem("s_inv")
        s_xor = sem("s_xor")
        s_xs = sem("s_xs")
        s_gd = sem("s_gd")
        s_vd = sem("s_vd")
        s_dve = sem("s_dve")

        s_badp = sem("s_badp")

        UNITS = B * NC * G

        with nc.Block() as block:
            @block.sync
            def _(sp):
                def load_x(b, c):
                    sp.dma_start(xn[:, b * NT + c * TPC:b * NT + (c + 1) * TPC, :],
                                 x_t[b, :, c * TPC:(c + 1) * TPC, :]).then_inc(s_xin[b * NC + c], 16)

                sp.dma_start(cond_rows, cond.rearrange("b (g p) -> (b g) p", p=P)).then_inc(s_cond, 16)
                for g in range(G):
                    sp.dma_start(xn[:, 0:TPC, g * P:(g + 1) * P],
                                 x_t[0, :, 0:TPC, g * P:(g + 1) * P]).then_inc(s_xfirst[g], 16)
                sp.dma_start(row0, row0_words.to_broadcast([P, SEQ // 4])).then_inc(s_row0, 16)

                def load_mask(q):
                    n = NT * (SEQ // 4) // NC
                    sp.dma_start(masks[:, q * n:(q + 1) * n], mask_words[:, q * n:(q + 1) * n]).then_inc(s_mask[q], 16)

                sp.dma_start(wstage, w_rows(wt)).then_inc(s_wt, 16)
                load_mask(0)
                sp.dma_start(wq_sb, w_rows(wq)).then_inc(s_wq, 16)
                load_x(0, 1)
                load_mask(1)
                load_mask(2)
                load_x(0, 2)
                load_mask(3)
                load_x(0, 3)
                sp.dma_start(wk_sb[:, :, :], w_rows(wk)).then_inc(s_wk, 16)
                for c in range(NC):
                    sp.dma_start(mask0[slab(c), :], mask[0:1, c * CHUNK:(c + 1) * CHUNK]
                                 .to_broadcast([SLAB, CHUNK])).then_inc(s_mrow, 16)
                sp.wait_ge(s_bk, USE_WT + G)
                sp.dma_start(wstage, w_rows(wv)).then_inc(s_wv, 16)
                sp.wait_ge(s_bk, USE_WV + G)
                sp.dma_start(wstage, w_rows(wo)).then_inc(s_wo, 16)
                for c in range(NC):
                    sp.wait_ge(s_xs, c + 1)
                    load_x(1, c)
                for q in range(NC):
                    sp.wait_ge(s_add, (q + 1) * TPC)
                    sp.dma_start(out_t[0, :, q * TPC:(q + 1) * TPC, :],
                                 xn[:, q * TPC:(q + 1) * TPC, :]).then_inc(s_out, 16)
                for t0 in [0] + list(range(1, NT, 2)):
                    t1 = min(t0 + 1 if t0 == 0 else t0 + 2, NT)
                    sp.wait_ge(s_add2, (t1 + 1) // 2)
                    sp.wait_ge(s_add, NT + t1 // 2)
                    sp.dma_start(out_t[1, :, t0:t1, :], xn[:, NT + t0:NT + t1, :]).then_inc(s_out, 16)
                sp.wait_ge(s_out, 16 * (NC + 1 + NT // 2))

            @block.gpsimd
            def _(pool):
                nc.gpsimd.memset(ident[:, :], 0.0).then_inc(s_const, 1)
                pool.wait_ge(s_const, 1)
                nc.gpsimd.affine_select(out=ident[:, :], in_=ident[:, :], compare_op=ALU.not_equal, fill=1.0,
                                        base=0, pattern=[[-1, P]], channel_multiplier=1).then_inc(s_const, 1)
                nc.gpsimd.memset(ones[:, :], 1.0).then_inc(s_const, 1)
                nc.gpsimd.iota(all_bits[:, :], pattern=[[0, 1]], base=-1, channel_multiplier=0).then_inc(s_bits, 1)
                nc.gpsimd.iota(left_ii, pattern=[[-1, CHUNK + 2]], base=CHUNK, channel_multiplier=0).then_inc(s_iota, 1)
                pool.wait_ge(s_iota, 1)
                nc.gpsimd.tensor_copy(left, left_ii).then_inc(s_steps, 1)
                nc.gpsimd.memset(headmask[:, :], 0.0)
                nc.gpsimd.memset(U[:, :, :, :], 0.0)
                nc.gpsimd.memset(vec[:, :, :, :], 0.0)
                nc.gpsimd.memset(w_sb[:, :, :], 0.0).then_inc(s_const, 1)
                pool.wait_ge(s_const, 4)
                nc.gpsimd.memset(headmask[:, 0:HG], 1.0).then_inc(s_const, 1)
                pool.wait_ge(s_const, 5)
                nc.gpsimd.affine_select(out=headmask[:, 0:HG], in_=headmask[:, 0:HG], compare_op=ALU.is_ge, fill=0.0,
                                        base=0, pattern=[[-E, HG]], channel_multiplier=1).then_inc(s_const, 1)
                pool.wait_ge(s_const, 6)
                nc.gpsimd.affine_select(out=headmask[:, 0:HG], in_=headmask[:, 0:HG], compare_op=ALU.is_gt, fill=0.0,
                                        base=E, pattern=[[E, HG]], channel_multiplier=-1).then_inc(s_const, 1)

                def fill(b):
                    if b == 0:
                        pool.wait_ge(s_condT, 1)
                    else:
                        pool.wait_ge(s_pp, b)
                    nc.gpsimd.memset(prob, NEG).then_inc(s_neg, 1)

                def add_rows(b):
                    pool.wait_ge(s_orow, b + 1)
                    for t in range(NT):
                        if b == 0 or t % 2 == 1:
                            nc.gpsimd.tensor_tensor(xn[:, b * NT + t, :], xn[:, b * NT + t, :], orow,
                                                    ALU.add).then_inc(s_add, 1)

                def unit_picks(b, c):
                    for g in range(G):
                        u = (b * NC + c) * G + g
                        pool.wait_ge(s_path, u + 1)
                        pool.wait_ge(s_hot, u + 1)
                        nc.gpsimd.tensor_tensor(rate2[:, g, 1:2 * CHUNK:2], spikes[:, g, 0:CHUNK],
                                                rate2[:, g, 0:2 * CHUNK:2], ALU.mult).then_inc(s_rs, 1)
                        if g < pool_v(b * NC + c):
                            v = (b * NC + c) * POOL_V + g
                            if v:
                                pool.wait_ge(s_vpre, v)
                            nc.gpsimd.tensor_tensor(picked, spikes[:, g, 0:CHUNK + 1], path[:, g, 1:PATH:2],
                                                    ALU.mult).then_inc(s_pick, 1)

                def unit_spikes(b, c, units):
                    for g in range(units):
                        u = (b * NC + c) * G + g
                        pool.wait_ge(s_xT, u + 1)
                        pool.wait_ge(s_height, u + 1)
                        xs = xT[:, chunk_slot(b, c), g, :]
                        nc.gpsimd.tensor_tensor(xs, xs, spikes[:, g, 0:CHUNK], ALU.add).then_inc(s_x1T, 1)

                def compare_masks(q):
                    pool.wait_ge(s_mask[q], 16)
                    pool.wait_ge(s_inv, 1)
                    words = masks.rearrange("p (r w) -> p r w", r=NT)[:, q * TPC:(q + 1) * TPC, :]
                    nc.gpsimd.tensor_tensor(words, words, row0.unsqueeze(1).to_broadcast([P, TPC, SEQ // 4]),
                                            ALU.add).then_inc(s_xor, 1)

                fill(0)
                for b in range(B):
                    for c in range(NC):
                        unit_picks(b, c)
                        if b == 0:
                            compare_masks(c)
                        unit_spikes(b, c, POOL_LAST if (b, c) == (B - 1, NC - 1) else G)
                        if (b, c) == (1, 2):
                            fill(1)
                add_rows(0)
                add_rows(1)

            @block.scalar
            def _(act):
                def bank_evict(use, dst):
                    act.wait_ge(s_bk, use + 1)
                    nc.scalar.copy(dst, pbk[use % 2][:, :]).then_inc(s_bkout, 1)

                def weight_evict(dst, use):
                    for k in range(G):
                        bank_evict(use + k, dst[:, k, :])

                def unit_evict(b, c):
                    for g in range(G):
                        u = (b * NC + c) * G + g
                        act.wait_ge(s_pin, u + 1)
                        if u >= G:
                            act.wait_ge(s_late, u - G + 1)
                            act.wait_ge(s_rs, u - G + 1)
                        nc.scalar.activation(rate2[:, g, :].rearrange("p (n two) -> p n two", two=2),
                                             pin[u % 2][:, :].unsqueeze(2).to_broadcast([P, CHUNK, 2]),
                                             ACT.Relu, scale=DT).then_inc(s_rate, 1)
                        if g == 0 and b * NC + c == SLOTS:
                            act.wait_ge(s_sp, 1)
                        if g == 0 and b * NC + c == SLOTS - 3:
                            act.wait_ge(s_tp, 1)
                        nc.scalar.copy(xT[:, chunk_slot(b, c), g, :], pin[u % 2][:, :]).then_inc(s_xT, 1)

                def unit_sums(b, c, first=0, end=G):
                    for g in range(first, end):
                        u = (b * NC + c) * G + g
                        act.wait_ge(s_rs, u + 1)
                        if u:
                            act.wait_ge(s_rst, u)
                        hot = rate2[:, g, 1:2 * CHUNK:2]
                        nc.scalar.activation(hot, hot, ACT.Copy,
                                             accum_out=rstar[:, b * NC + c, g:g + 1]).then_inc(s_rst, 1)
                        if g < pool_v(b * NC + c):
                            v = (b * NC + c) * POOL_V + g
                            act.wait_ge(s_pick, v + 1)
                            if v:
                                act.wait_ge(s_vpre, v)
                            nc.scalar.activation(picked, picked, ACT.Copy,
                                                 accum_out=vprev[:, g:g + 1]).then_inc(s_vpre, 1)

                def spike_heights(b, c, units):
                    act.wait_ge(s_spk, b * NC + c + 1)
                    for g in range(units):
                        nc.scalar.activation(spikes[:, g, 0:CHUNK], spikes[:, g, 0:CHUNK], ACT.Relu,
                                             scale=spk[:, g:g + 1]).then_inc(s_height, 1)

                def back_evict(b, c, first=0, end=TPC):
                    for t in range(first, end):
                        bank_evict(use_back(b * NC + c) + t, xn[:, b * NT + c * TPC + t, :])

                def A_evict(b, c):
                    n = b * NC + c
                    act.wait_ge(s_Ar, n + 1)
                    nc.scalar.copy(A_rows[:, :], pAP[:, 0:P]).then_inc(s_Are, 1)
                    act.wait_ge(s_Ap, n + 1)
                    if n >= 2:
                        act.wait_ge(s_Yc, n - 1)
                    nc.scalar.copy(A_sb[:, n % 2, :, :], pAP[:, P:2 * P].rearrange("p (t h) -> p t h", t=TPC)
                                   ).then_inc(s_A, 1)

                def by_group(x):
                    return x.rearrange("p k (j h) -> p k j h", j=G)

                def mid_y_rows(b):
                    act.wait_ge(s_Yc, NC * (b + 1))
                    nc.scalar.copy(rows[:, :], pY[:, :]).then_inc(s_Ye, 1)

                def mid_y_cols(b):
                    act.wait_ge(s_yc, b + 1)
                    nc.scalar.copy(vec[:, :, :, 0:HG], by_group(ps_comb[:, :, 0:H])).then_inc(s_y, 1)

                def mid_y_heads(b):
                    act.wait_ge(s_qp, b + 1)
                    nc.scalar.copy(he_rows[:, :], ps_rows).then_inc(s_qe, 1)

                def mid_w(b):
                    act.wait_ge(s_wp, b + 1)
                    nc.scalar.mul(rows[:, :], pY[:, :], SCALE).then_inc(s_wr, 1)
                    act.wait_ge(s_wtr, b + 1)
                    nc.scalar.copy(by_group(w_sb[:, :, 0:H]), pS[:, :].rearrange(
                        "p (k j h) -> p k j h", k=G, j=G)[:, :, :, 0:HG]).then_inc(s_w, 1)

                def mid_exp(b):
                    act.wait_ge(s_mx, b + 1)
                    nc.scalar.activation(prob, prob, ACT.Exp, bias=nmx[:, :],
                                         accum_out=psum_rows[:, :]).then_inc(s_ex, 1)
                    act.wait_ge(s_pp, b + 1)
                    nc.scalar.copy(pT[:, :, :], pY[:, :].rearrange("p (t n) -> p t n", t=TPC)).then_inc(s_pT, 1)

                def mid_part(b):
                    act.wait_ge(s_mb, b + 1)
                    nc.scalar.activation(part[:, :], ps_mcol, ACT.Exp, bias=mx[:, :], scale=-1.0).then_inc(s_f, 1)

                def mid_z_rows(b):
                    act.wait_ge(s_zp, b + 1)
                    nc.scalar.copy(rows[:, :], pS[:, :]).then_inc(s_ze, 1)

                def mid_z_cols(b):
                    act.wait_ge(s_zc, b + 1)
                    nc.scalar.copy(vec[:, :, :, 0:HG], by_group(ps_comb[:, :, 0:H])).then_inc(s_z, 1)

                def mid_z_heads(b):
                    act.wait_ge(s_op, b + 1)
                    nc.scalar.copy(he_rows[:, :], ps_rows).then_inc(s_oe, 1)

                def mid_row_parts(b):
                    act.wait_ge(s_ypp, b + 1)
                    nc.scalar.copy(row_parts, pS[:, :]).then_inc(s_ype, 1)

                def mid_row(b):
                    act.wait_ge(s_yp, b + 1)
                    if b:
                        act.wait_ge(s_add, NT)
                    nc.scalar.copy(orow, pS[:, :]).then_inc(s_orow, 1)

                def square_masks(q):
                    n = NT * (SEQ // 4) // NC
                    act.wait_ge(s_xor, q + 1)
                    nc.scalar.activation(masks_f[:, q * n:(q + 1) * n], masks[:, q * n:(q + 1) * n], ACT.Square,
                                         bias=ones[:, :],
                                         accum_out=xorsum[:, q:q + 1]).then_inc(s_xs, 1)

                act.wait_ge(s_condT, 1)
                cols = pM[:, 0:B * G].rearrange("p (b g) -> p b g", b=B)
                nc.scalar.copy(vinit[:, :, :], cols).then_inc(s_vinit, 1)
                nc.scalar.copy(tcol[:, :, :], cols.rearrange("p b g -> p g b")).then_inc(s_tcol, 1)
                unit_evict(0, 0)
                weight_evict(wtT, USE_WT)
                unit_sums(0, 0)
                unit_evict(0, 1)
                spike_heights(0, 0, G)
                weight_evict(wqT, USE_WQ)
                square_masks(0)
                unit_sums(0, 1)
                unit_evict(0, 2)
                spike_heights(0, 1, G)
                weight_evict(wvT, USE_WV)
                A_evict(0, 0)
                back_evict(0, 0)
                unit_sums(0, 2)
                unit_evict(0, 3)
                spike_heights(0, 2, G)
                weight_evict(woT, USE_WO)
                A_evict(0, 1)
                back_evict(0, 1)
                unit_sums(0, 3)
                unit_evict(1, 0)
                spike_heights(0, 3, G)
                A_evict(0, 2)
                back_evict(0, 2)
                square_masks(1)
                square_masks(2)
                A_evict(0, 3)
                unit_sums(1, 0, 0, 1)
                back_evict(0, 3)
                unit_sums(1, 0, 1, 2)
                mid_y_rows(0)
                unit_sums(1, 0, 2, G)
                mid_y_cols(0)
                mid_y_heads(0)
                unit_evict(1, 1)
                spike_heights(1, 0, G)
                square_masks(3)
                mid_w(0)
                unit_sums(1, 1)
                mid_exp(0)
                unit_evict(1, 2)
                spike_heights(1, 1, G)
                A_evict(1, 0)
                back_evict(1, 0)
                mid_part(0)
                unit_sums(1, 2)
                mid_z_rows(0)
                unit_evict(1, 3)
                spike_heights(1, 2, G)
                A_evict(1, 1)
                back_evict(1, 1)
                mid_z_cols(0)
                unit_sums(1, 3, 0, 2)
                mid_z_heads(0)
                unit_sums(1, 3, 2, G)
                A_evict(1, 2)
                back_evict(1, 2, 0, 2)
                spike_heights(1, 3, POOL_LAST)
                back_evict(1, 2, 2, TPC)
                A_evict(1, 3)
                back_evict(1, 3)
                mid_y_rows(1)
                mid_row_parts(0)
                mid_y_cols(1)
                mid_y_heads(1)
                mid_row(0)
                mid_w(1)
                mid_exp(1)
                mid_part(1)
                mid_z_rows(1)
                mid_z_cols(1)
                mid_z_heads(1)
                mid_row_parts(1)
                mid_row(1)

            @block.vector
            def _(dve):
                n = [0]

                def link(ins):
                    n[0] += 1
                    ins.then_inc(s_dve, 1)
                    dve.wait_ge(s_dve, n[0])

                def mark(ins):
                    n[0] += 1
                    ins.then_inc(s_dve, 1)

                def catch_up():
                    dve.wait_ge(s_dve, n[0])

                def chunk(b, c):
                    k = b * NC + c
                    u0 = k * G
                    cn = cnt[:, k % 2, :]
                    picked_by_pool = pool_v(k)

                    starts = vinit[:, b, :] if c == 0 else vend[:, k - 1, :]

                    def scan_path(g):
                        if g == 0 or g == 2:
                            catch_up()
                        dve.wait_ge(s_rate, u0 + g + 1)
                        nc.vector.tensor_tensor_scan(path[:, g, 2:PATH], rate2[:, g, :], rate2[:, g, :],
                                                     starts[:, g:g + 1], ALU.add, ALU.add).then_inc(s_path, 1)

                    def count(g):
                        dve.wait_ge(s_path, u0 + g + 1)
                        if u0 + g:
                            dve.wait_ge(s_cnt, u0 + g)
                        nc.vector.tensor_scalar(junk[:, 0:CHUNK], path[:, g, 3:PATH:2], 1.0, None, ALU.is_ge,
                                                ALU.add, accum_out=cn[:, g:g + 1]).then_inc(s_cnt, 1)

                    def mark_step(g):
                        dve.wait_ge(s_cnt, u0 + g + 1)
                        if k:
                            dve.wait_ge(s_x1T, u0 - G + g + 1)
                        nc.vector.tensor_scalar(spikes[:, g, :], left[:, :], cn[:, g:g + 1], None,
                                                ALU.is_equal).then_inc(s_hot, 1)

                    def voltage_before(g):
                        begins = path[:, g, 1:PATH:2]
                        mark(nc.vector.scalar_tensor_tensor(begins, left[:, 0:CHUNK + 1], cn[:, g:g + 1], begins,
                                                            ALU.is_equal, ALU.mult, accum_out=vprev[:, g:g + 1]))

                    def rates_after(g):
                        if g < picked_by_pool:
                            dve.wait_ge(s_pick, k * POOL_V + g + 1)
                        else:
                            catch_up()
                        nc.vector.scalar_tensor_tensor(
                            late[:, g, :].rearrange("p (n two) -> p n two", two=2),
                            left[:, 0:CHUNK].unsqueeze(2).to_broadcast([P, CHUNK, 2]), cn[:, g:g + 1],
                            rate2[:, g, 0:2 * CHUNK:2].unsqueeze(2).to_broadcast([P, CHUNK, 2]), ALU.is_lt,
                            ALU.mult).then_inc(s_late, 1)

                    def spiking_step():
                        rs = rstar[:, k, :]
                        dve.wait_ge(s_rst, u0 + G)
                        if picked_by_pool:
                            dve.wait_ge(s_vpre, (k + 1) * POOL_V)
                        catch_up()
                        mark(nc.vector.tensor_tensor(vpre[:, :], vprev[:, :], rs, ALU.add))
                        for _ in range(SUB - 1):
                            catch_up()
                            link(nc.vector.scalar_tensor_tensor(nvlt[:, :], vpre[:, :], 1.0, vpre[:, :], ALU.is_ge,
                                                                ALU.subtract))
                            mark(nc.vector.tensor_tensor(vpre[:, :], rs, nvlt[:, :], ALU.subtract))
                        catch_up()
                        mark(nc.vector.scalar_tensor_tensor(nvlt[:, :], vpre[:, :], 1.0, vpre[:, :], ALU.is_ge,
                                                            ALU.subtract))
                        if k:
                            dve.wait_ge(s_height, u0)
                        nc.vector.tensor_scalar(spk[:, :], vpre[:, :], 1.0, PER_SPIKE, ALU.is_ge,
                                                ALU.mult).then_inc(s_spk, 1)
                        catch_up()
                        mark(nc.vector.tensor_scalar(vstar[:, :], nvlt[:, :], -1.0, None, ALU.mult))

                    def scan_rest():
                        def keep_ends(first, end):
                            mark(nc.vector.tensor_copy(vend[:, k, first:end], late[:, first:end, 2 * CHUNK - 1]))

                        catch_up()
                        dve.wait_ge(s_late, u0 + G)
                        for g in range(G):
                            mark(nc.vector.tensor_tensor_scan(late[:, g, :], late[:, g, :], late[:, g, :],
                                                              vstar[:, g:g + 1], ALU.add, ALU.add))
                            if g == G - 2:
                                dve.wait_ge(s_dve, n[0] - 1)
                                keep_ends(0, G - 2)
                        catch_up()
                        keep_ends(G - 2, G)

                    if k == 0:
                        dve.wait_ge(s_vinit, 1)
                    scan_path(0)
                    scan_path(1)
                    mark(nc.vector.tensor_copy(path[:, :, 1], starts))
                    count(0)
                    for g in range(2, G):
                        scan_path(g)
                        mark_step(g - 2)
                        count(g - 1)
                    between(b, c, 0)
                    mark_step(G - 2)
                    count(G - 1)
                    mark_step(G - 1)
                    for g in range(picked_by_pool, G):
                        voltage_before(g)
                    if k < B * NC - 1:
                        for g in range(G):
                            rates_after(g)
                        between(b, c, 1)
                        spiking_step()
                        scan_rest()
                        between(b, c, 2)
                    else:
                        spiking_step()
                        last_spikes(b, c)
                        between(b, c, 1)
                        for g in range(G):
                            rates_after(g)
                        scan_rest()
                        catch_up()

                def last_spikes(b, c):
                    dve.wait_ge(s_spk, b * NC + c + 1)
                    for g in range(POOL_LAST, G):
                        u = (b * NC + c) * G + g
                        dve.wait_ge(s_rs, u + 1)
                        dve.wait_ge(s_xT, u + 1)
                        xs = xT[:, chunk_slot(b, c), g, :]
                        nc.vector.scalar_tensor_tensor(xs, spikes[:, g, 0:CHUNK], spk[:, g:g + 1], xs, ALU.mult,
                                                       ALU.add).then_inc(s_x1L, 1)

                def time_vector():
                    dve.wait_ge(s_tp, 1)
                    dve.wait_ge(s_const, 7)
                    for b in range(B):
                        nc.vector.tensor_tensor(tpd[:, :, b, :],
                                                ps_tp[:, :, b].unsqueeze(2).to_broadcast([P, G, HG]), hm_b(),
                                                ALU.mult).then_inc(s_tpd, 1)

                def time_products():
                    dve.wait_ge(s_Up, 1)
                    nc.vector.tensor_copy(U[:, :, :, 0:H], ps_U).then_inc(s_U, 1)

                def complement_row0():
                    dve.wait_ge(s_row0, 16)
                    dve.wait_ge(s_bits, 1)
                    nc.vector.tensor_tensor(row0, row0, all_bits[:, :].to_broadcast([P, SEQ // 4]),
                                            ALU.bitwise_xor).then_inc(s_inv, 1)

                def mid_q(b):
                    dve.wait_ge(s_qt, b + 1)
                    nc.vector.tensor_tensor(qsel[:, :, :], ps_cols, hm_slab(), ALU.mult).then_inc(s_q, 1)

                def mid_scores(b):
                    dve.wait_ge(s_neg, b + 1)
                    dve.wait_ge(s_mrow, 16 * NC)
                    dve.wait_ge(s_sp, b + 1)
                    nc.vector.copy_predicated(prob, mask0, pS[:, :]).then_inc(s_sc, 1)
                    dve.wait_ge(s_sc, b + 1)
                    link(nc.vector.reduce_max(mx[:, :], prob, AX))
                    nc.vector.tensor_scalar(nmx[:, :], mx[:, :], -1.0, None, ALU.mult).then_inc(s_mx, 1)

                def mid_max(b):
                    dve.wait_ge(s_mt, b + 1)
                    link(nc.vector.reduce_max(mrow, ps_mrow.rearrange("o (c h) -> o h c", c=G), AX))
                    nc.vector.tensor_copy(mrow_all, mrow.unsqueeze(1).to_broadcast([1, G, SLAB])
                                          ).then_inc(s_mr, 1)

                def mid_share(b):
                    dve.wait_ge(s_f, b + 1)
                    nc.vector.tensor_tensor(share[:, :], part[:, :], psum_rows[:, :], ALU.mult).then_inc(s_sh, 1)

                def mid_comb(b):
                    dve.wait_ge(s_tot, b + 1)
                    link(nc.vector.reciprocal(rtot[:, :], ps_tot))
                    nc.vector.tensor_scalar(comb[:, :], same[:, :], part[:, :], rtot[:, :], ALU.mult,
                                            ALU.mult).then_inc(s_cb, 1)

                def mid_o(b):
                    dve.wait_ge(s_ot, b + 1)
                    link(nc.vector.tensor_tensor(osel[:, :, :], ps_cols, hm_slab(), ALU.mult))
                    nc.vector.reduce_sum(ocol[:, :], osel[:, :, :], AX).then_inc(s_o, 1)

                def between(b, c, point):
                    at = (b, c, point)
                    if at == (0, 0, 0):
                        complement_row0()
                    elif at == (0, 0, 2):
                        time_vector()
                    elif at == (0, 1, 1):
                        time_products()
                    elif at == (1, 0, 2):
                        mid_q(0)
                    elif at == (1, 1, 1):
                        mid_scores(0)
                    elif at == (1, 1, 2):
                        mid_max(0)
                    elif at == (1, 2, 1):
                        mid_share(0)
                    elif at == (1, 2, 2):
                        mid_comb(0)
                    elif at == (1, 3, 1):
                        mid_o(0)

                dve.wait_ge(s_const, 3)
                nc.vector.reduce_sum(same[:, :], ident[:, :].rearrange("p (i h) -> p h i", i=G), AX).then_inc(s_same, 1)
                dve.wait_ge(s_same, 1)
                nc.vector.tensor_copy(same_all[:, :, :], same[:, :].unsqueeze(1).to_broadcast([P, G, SLAB])
                                      ).then_inc(s_same, 1)
                dve.wait_ge(s_steps, 1)
                for b in range(B):
                    for c in range(NC):
                        chunk(b, c)
                mid_q(1)
                link(nc.vector.tensor_scalar(junk[:, 0:B * G], vinit[:, :, :].rearrange("p b g -> p (b g)"), 1.0,
                                             None, ALU.is_lt))
                link(nc.vector.tensor_reduce(good[:, 0:1], junk[:, 0:B * G], AX, ALU.min))
                link(nc.vector.tensor_scalar(junk[:, 0:UNITS], rstar[:, :, :].rearrange("p k g -> p (k g)"), 1.0,
                                             None, ALU.is_lt))
                link(nc.vector.tensor_reduce(good[:, 1:2], junk[:, 0:UNITS], AX, ALU.min))
                link(nc.vector.tensor_scalar(junk[:, 0:UNITS], vend[:, :, :].rearrange("p k g -> p (k g)"), 1.0,
                                             None, ALU.is_lt))
                link(nc.vector.tensor_reduce(good[:, 2:3], junk[:, 0:UNITS], AX, ALU.min))
                dve.wait_ge(s_xs, NC)
                link(nc.vector.tensor_scalar(junk[:, 0:NC], xorsum[:, :], 0.0, None, ALU.is_equal))
                link(nc.vector.tensor_reduce(good[:, 3:4], junk[:, 0:NC], AX, ALU.min))
                nc.vector.tensor_reduce(goodall[:, :], good[:, :], AX, ALU.min).then_inc(s_gd, 1)
                mid_scores(1)
                mid_max(1)
                mid_share(1)
                mid_comb(1)
                mid_o(1)
                dve.wait_ge(s_badp, 1)
                nc.vector.tensor_scalar(verdict[:, :], ps_bad, FORCE or P - 0.5, None,
                                        ALU.is_lt).then_inc(s_vd, 1)
                dve.wait_ge(s_orow, B)
                for t in range(0, NT, 2):
                    nc.vector.tensor_tensor(xn[:, NT + t, :], xn[:, NT + t, :], orow, ALU.add).then_inc(s_add2, 1)

            @block.tensor
            def _(pe):
                def keep_busy(b, n):
                    if b == B - 1:
                        for _ in range(n):
                            nc.tensor.transpose(pin[0][:, 0:P], ident[:, :], ident[:, :])

                def bank_fill(use, src):
                    if use >= 2:
                        pe.wait_ge(s_bkout, use - 1)
                    return pe_transpose_tile(pbk[use % 2], src).then_inc(s_bk, 1)

                def weight(w, use):
                    for k in range(G):
                        bank_fill(use + k, [w[:, j, k * P:(k + 1) * P] for j in range(G)])

                def unit_in(b, c):
                    if b * NC + c:
                        pe.wait_ge(s_xin[b * NC + c], 16)
                    for g in range(G):
                        if b * NC + c == 0:
                            pe.wait_ge(s_xfirst[g], 16)
                        u = (b * NC + c) * G + g
                        if u >= 2:
                            pe.wait_ge(s_xT, u - 1)
                        pe_transpose_tile(pin[u % 2], [xn[:, b * NT + c * TPC + t, g * P:(g + 1) * P]
                                                       for t in range(TPC)]).then_inc(s_pin, 1)

                def back_A(b, c):
                    k = b * NC + c
                    if k == B * NC - 1:
                        pe.wait_ge(s_x1T, k * G + POOL_LAST)
                        pe.wait_ge(s_x1L, G - POOL_LAST)
                    else:
                        pe.wait_ge(s_x1T, (k + 1) * G)
                    if k == 0:
                        pe.wait_ge(s_U, 1)
                    if k > 0:
                        pe.wait_ge(s_A, k)
                    pe_A(b, chunk_slot(b, c)).then_inc(s_Ar, 1)

                def back_tiles(b, c):
                    k = b * NC + c
                    slot = chunk_slot(b, c)
                    bank_fill(use_back(k), [xT[:, slot, g, 0:P] for g in range(G)])
                    pe.wait_ge(s_Are, k + 1)
                    nc.tensor.transpose(pAP[:, P:2 * P], A_rows[:, :], ident[:, :]).then_inc(s_Ap, 1)
                    for t in range(1, TPC):
                        bank_fill(use_back(k) + t, [xT[:, slot, g, t * P:(t + 1) * P] for g in range(G)])

                def back_Y(b, c):
                    k = b * NC + c
                    pe.wait_ge(s_A, k + 1)
                    pe.wait_ge(s_bkout, use_back(k) + TPC)
                    if k == NC:
                        pe.wait_ge(s_pT, 1)
                    pe_Y(b, c, k % 2).then_inc(s_Yc, 1)

                def back(b, c):
                    back_A(b, c)
                    back_tiles(b, c)
                    back_Y(b, c)

                def mid_y(b):
                    pe.wait_ge(s_Ye, b + 1)
                    pe.wait_ge(s_same, 2)
                    pe_combine(same[:, :]).then_inc(s_yc, 1)
                    if b:
                        row_sum(b - 1)
                    pe.wait_ge(s_y, b + 1)
                    pe_heads(wqT).then_inc(s_qp, 1)
                    keep_busy(b, 3)
                    pe.wait_ge(s_qe, b + 1)
                    nc.tensor.transpose(pM[:, P:2 * P], he_rows[:, :], ident[:, :]).then_inc(s_qt, 1)

                def mid_w(b):
                    keep_busy(b, 3)
                    pe.wait_ge(s_q, b + 1)
                    pe.wait_ge(s_wk, 16)
                    pe_w().then_inc(s_wp, 1)
                    keep_busy(b, 6)
                    pe.wait_ge(s_wr, b + 1)
                    if b:
                        pe.wait_ge(s_orow, b)
                    pe_transpose_tile(pS, [rows[:, k * P:(k + 1) * P] for k in range(G)]).then_inc(s_wtr, 1)
                    keep_busy(b, 3)
                    pe.wait_ge(s_w, b + 1)
                    pe_scores(b).then_inc(s_sp, 1)

                def mid_exp(b):
                    keep_busy(b, 14)
                    pe.wait_ge(s_mx, b + 1)
                    nc.tensor.transpose(ps_mrow, mx[:, :], ident[:, :]).then_inc(s_mt, 1)
                    keep_busy(b, 4)
                    pe.wait_ge(s_ex, b + 1)
                    pe_transpose_tile(pY, [prob[:, t * P:(t + 1) * P] for t in range(TPC)]).then_inc(s_pp, 1)

                def mid_sum(b):
                    pe.wait_ge(s_mr, b + 1)
                    nc.tensor.matmul(ps_mcol, mrow_all.rearrange("o c h -> o (c h)"), ident[0:1, 0:1],
                                     start=True, stop=True).then_inc(s_mb, 1)
                    keep_busy(b, 5)
                    pe.wait_ge(s_pT, b + 1)
                    pe_z(b).then_inc(s_zp, 1)

                def mid_tot(b):
                    pe.wait_ge(s_sh, b + 1)
                    nc.tensor.matmul(ps_tot, same_all[:, :, :].rearrange("p c h -> p (c h)"), share[:, :],
                                     start=True, stop=True).then_inc(s_tot, 1)

                def mid_z(b):
                    keep_busy(b, 5)
                    pe.wait_ge(s_cb, b + 1)
                    pe.wait_ge(s_ze, b + 1)
                    pe_combine(comb[:, :]).then_inc(s_zc, 1)
                    keep_busy(b, 3)
                    pe.wait_ge(s_z, b + 1)
                    pe_heads(wvT).then_inc(s_op, 1)
                    keep_busy(b, 3)
                    pe.wait_ge(s_oe, b + 1)
                    nc.tensor.transpose(pM[:, P:2 * P], he_rows[:, :], ident[:, :]).then_inc(s_ot, 1)

                def pe_row_parts(b):
                    keep_busy(b, 6)
                    pe.wait_ge(s_o, b + 1)
                    for j in range(G):
                        last = nc.tensor.matmul(pS[slab(j), :], ocol[:, j:j + 1].to_broadcast([P, SLAB]), woT[:, j, :],
                                                start=True, stop=True)
                    last.then_inc(s_ypp, 1)

                def row_sum(b):
                    keep_busy(b, 7)
                    pe.wait_ge(s_ype, b + 1)
                    nc.tensor.matmul(pS[:, :], same[:, 0:1].to_broadcast([P, P]), row_parts,
                                     start=True, stop=True).then_inc(s_yp, 1)

                pe.wait_ge(s_const, 2)
                pe.wait_ge(s_cond, 16)
                nc.tensor.transpose(pM[:, 0:B * G], cond_rows, ident[0:B * G, 0:B * G]).then_inc(s_condT, 1)
                unit_in(0, 0)
                pe.wait_ge(s_const, 7)
                pe.wait_ge(s_wt, 16)
                weight(wstage, USE_WT)
                pe.wait_ge(s_bkout, USE_WT + G)
                pe.wait_ge(s_tcol, 1)
                for j in range(G):
                    for k in range(G):
                        last = nc.tensor.matmul(ps_tp[:, j, :], wtT[:, k, j * P:(j + 1) * P], tcol[:, k, :],
                                                start=(k == 0), stop=(k == G - 1))
                last.then_inc(s_tp, 1)
                unit_in(0, 1)
                pe.wait_ge(s_wq, 16)
                weight(wq_sb, USE_WQ)
                pe.wait_ge(s_tpd, B)
                for k in range(G):
                    for j in range(G):
                        last = nc.tensor.matmul(ps_U[:, k, :, j * HG:(j + 1) * HG], wq_sb[:, j, k * P:(k + 1) * P],
                                                tpd[:, j, :, :], start=True, stop=True)
                last.then_inc(s_Up, 1)
                unit_in(0, 2)
                pe.wait_ge(s_wv, 16)
                weight(wstage, USE_WV)
                back(0, 0)
                unit_in(0, 3)
                pe.wait_ge(s_wo, 16)
                weight(wstage, USE_WO)
                back(0, 1)
                unit_in(1, 0)
                back(0, 2)
                back(0, 3)
                mid_y(0)
                unit_in(1, 1)
                mid_w(0)
                mid_exp(0)
                unit_in(1, 2)
                back(1, 0)
                mid_sum(0)
                unit_in(1, 3)
                mid_tot(0)
                back(1, 1)
                mid_z(0)
                back_A(1, 2)
                back_tiles(1, 2)
                back_A(1, 3)
                back_Y(1, 2)
                back_tiles(1, 3)
                back_Y(1, 3)
                pe_row_parts(0)
                mid_y(1)
                mid_w(1)
                pe.wait_ge(s_gd, 1)
                nc.tensor.matmul(ps_bad, ones[:, :].to_broadcast([P, P]), goodall[:, :], start=True, stop=True).then_inc(s_badp, 1)
                mid_exp(1)
                mid_sum(1)
                mid_tot(1)
                mid_z(1)
                pe_row_parts(1)
                row_sum(1)

        sc = cut(SEQ, True)[0:H, :]
        sel = cut(H * P)[0:H, :]
        onehot = cut(P)[0:H, :]
        mrows = cut(SEQ // 4).bitcast(u8)
        S = cut(SEQ)
        ST = cut(SEQ)
        O = cut(D)
        OT = cut(D).rearrange("p (j n) -> p j n", j=G)
        res = cut(D)
        tile = cut(D).rearrange("p (g n) -> p g n", g=G)
        v, r, a, m, n0, f = [cut(G).rearrange("p (g n) -> p g n", g=G) for _ in range(6)]
        rowmax, nrowmax, rowsum, rrow = [cut(1) for _ in range(4)]
        gA = cut(TPC * H)
        gy = cut(G * H).rearrange("p (k h) -> p k h", k=G)
        gw = cut(G * H).rearrange("p (k h) -> p k h", k=G)
        gq = cut(G * HG).rearrange("p (j h) -> p j h", j=G)
        pscore = [pin[0], pin[1], pbk[0], pbk[1]]
        pturn = [pAP, pY, pS, pM]

        g_sel = sem("g_sel")
        g_ld = sem("g_ld")
        g_tp = sem("g_tp")
        g_ev = sem("g_ev")
        g_bt = sem("g_bt")
        g_btp = sem("g_btp")
        g_bev = sem("g_bev")
        g_A = sem("g_A")
        g_Ae = sem("g_Ae")
        g_Y = sem("g_Y")
        g_ye = sem("g_ye")
        g_q = sem("g_q")
        g_qe = sem("g_qe")
        g_w = sem("g_w")
        g_we = sem("g_we")
        g_s = sem("g_s")
        g_se = sem("g_se")
        g_v = sem("g_v")
        g_ve = sem("g_ve")
        g_mk = sem("g_mk")
        g_neg = sem("g_neg")
        g_oh = sem("g_oh")
        g_bc = sem("g_bc")
        g_cp = sem("g_cp")
        g_mx = sem("g_mx")
        g_ex = sem("g_ex")
        g_st = sem("g_st")
        g_ste = sem("g_ste")
        g_o = sem("g_o")
        g_O = sem("g_O")
        g_ot = sem("g_ot")
        g_ote = sem("g_ote")
        g_y = sem("g_y")
        g_res = sem("g_res")
        g_out = sem("g_out")
        g_dve = sem("g_dve")
        g_go = sem("g_go")
        g_sum = sem("g_sum")


        def pe_A_general(b, c):
            for t in range(TPC):
                for g in range(G):
                    last = nc.tensor.matmul(pAP[:, t * H:(t + 1) * H], xT[:, c, g, t * P:(t + 1) * P],
                                            U[:, g, b, 0:H], start=(g == 0), stop=(g == G - 1))
            return last

        def pe_Y_general(b, c):
            for t in range(TPC):
                for k in range(G):
                    last = nc.tensor.matmul(pY[:, k * H:(k + 1) * H], xn[:, b * NT + c * TPC + t, k * P:(k + 1) * P],
                                            gA[:, t * H:(t + 1) * H], start=(c == 0 and t == 0 and k == 0),
                                            stop=(c == NC - 1 and t == TPC - 1), skip_group_check=True)
            return last

        with nc.Block() as block:
            @block.sync
            def _(sp):
                bad = sp.value_load(verdict[0:1, 0:1])
                with sp.If(bad > 0):
                    sp.sem_inc(g_out, 16)
                    for b in range(B):
                        with sp.Fori(0, NT) as t:
                            sp.wait_ge(g_tp, t + (b * NT + 1))
                            sp.dma_start(tile, x_t[b, :, bass.ds(t, 1), :]
                                         .rearrange("p t (g n) -> p (t g) n", g=G)).then_inc(g_ld, 16)
                        with sp.Fori(0, NT) as t:
                            sp.wait_ge(g_res, t + (b * NT + 1))
                            sp.dma_start(mrows, mask[bass.ds(t * P, P), :]).then_inc(g_mk, 16)
                            sp.wait_ge(g_res, t + (b * NT + 2))
                            sp.dma_start(out_t[b, :, bass.ds(t, 1), :],
                                         res.unsqueeze(1)).then_inc(g_out, 16)
                    sp.wait_ge(g_out, 16 * (B * NT + 1))
                sp.end_ifs()

            @block.gpsimd
            def _(pool):
                bad = pool.value_load(verdict[0:1, 0:1])
                with pool.If(bad > 0):
                    nc.gpsimd.memset(sel, 1.0).then_inc(g_sel, 1)
                    pool.wait_ge(g_sel, 1)
                    nc.gpsimd.affine_select(out=sel, in_=sel, compare_op=ALU.is_ge, fill=0.0, base=0,
                                            pattern=[[1, H * P]], channel_multiplier=-P).then_inc(g_sel, 1)
                    pool.wait_ge(g_sel, 2)
                    nc.gpsimd.affine_select(out=sel, in_=sel, compare_op=ALU.is_gt, fill=0.0, base=P,
                                            pattern=[[-1, H * P]], channel_multiplier=P).then_inc(g_sel, 1)
                    with pool.Fori(0, B * NT * H) as i:
                        pool.wait_ge(g_st, i + 1)
                        pool.sem_inc(g_go, 1)
                        nc.gpsimd.memset(S, NEG).then_inc(g_neg, 1)
                pool.end_ifs()

            @block.scalar
            def _(act):
                bad = act.value_load(verdict[0:1, 0:1])
                with act.If(bad > 0):
                    act.sem_inc(g_ev, 1)
                    act.sem_inc(g_bev, 1)
                    for b in range(B):
                        with act.Fori(0, NC) as c:
                            with act.Fori(0, TPC) as t:
                                act.wait_ge(g_tp, c * TPC + t + (b * NT + 2))
                                nc.scalar.copy(xT[:, bass.ds(c, 1), :, bass.ds(t * P, P)],
                                               pin[0][:, :].rearrange("p (g n) -> p g n", g=G).unsqueeze(1)).then_inc(g_ev, 1)
                        with act.Fori(0, NT) as t:
                            act.wait_ge(g_btp, t + (b * NT + 2))
                            nc.scalar.copy(xn[:, bass.ds(t + b * NT, 1), :], pin[1][:, :].unsqueeze(1)).then_inc(g_bev, 1)
                        for c in range(NC):
                            k = b * NC + c
                            act.wait_ge(g_A, k + 1)
                            nc.scalar.copy(gA, pAP[:, 0:TPC * H]).then_inc(g_Ae, 1)
                        act.wait_ge(g_Y, NC * (b + 1))
                        nc.scalar.copy(gy, pY[:, 0:G * H].rearrange("p (k h) -> p k h", k=G)).then_inc(g_ye, 1)
                        act.wait_ge(g_w, b + 1)
                        nc.scalar.mul(gw, ps_w, SCALE).then_inc(g_we, 1)
                        for c in range(NC):
                            k = b * NC + c
                            act.wait_ge(g_s, k + 1)
                            nc.scalar.copy(sc[:, c * CHUNK:(c + 1) * CHUNK], pS[0:H, :]).then_inc(g_se, 1)
                        for t in range(NT):
                            i = b * NT + t
                            act.wait_ge(g_v, i + 1)
                            nc.scalar.copy(xT[:, t // TPC, :, (t % TPC) * P:(t % TPC + 1) * P],
                                           pbk[t % 2][:, :].rearrange("p (g n) -> p g n", g=G)).then_inc(g_ve, 1)
                        with act.Fori(0, NT) as t:
                            with act.Fori(0, H) as h:
                                i = t * H + h
                                act.wait_ge(g_mx, i + (b * NT * H + 1))
                                nc.scalar.activation(S, S, ACT.Exp, bias=nrowmax, accum_out=rowsum).then_inc(g_ex, 1)
                                act.wait_ge(g_st, i + (b * NT * H + 2))
                                for q in range(NC):
                                    nc.scalar.copy(ST[:, q * CHUNK:(q + 1) * CHUNK], pturn[q][:, :]).then_inc(g_ste, 1)
                            act.wait_ge(g_ot, t + (b * NT + 1))
                            nc.scalar.copy(OT, pin[1][:, :].rearrange("p (j n) -> p j n", j=G)).then_inc(g_ote, 1)
                act.end_ifs()

            @block.vector
            def _(dve):
                bad = dve.value_load(verdict[0:1, 0:1])
                with dve.If(bad > 0):
                    dve.sem_inc(g_res, 1)
                    dve.wait_ge(g_sel, 3)
                    OPS = 1 + SUB * 7 + 2
                    for b in range(B):
                        dve.wait_ge(g_ev, NT * (b + 1) + 1)
                        nc.vector.tensor_copy(v, vinit[:, b, :].unsqueeze(2)).then_inc(g_dve, 1)
                        with dve.Fori(0, NC) as c:
                            with dve.Fori(0, CHUNK) as s:
                                before = (c * CHUNK + s) * OPS + (b * (SEQ * OPS + 1) + 1)
                                done = [0]

                                def link(ins):
                                    ins.then_inc(g_dve, 1)
                                    done[0] += 1
                                    dve.wait_ge(g_dve, before + done[0])

                                xs = xT[:, bass.ds(c, 1), :, bass.ds(s, 1)].rearrange("p c g n -> p (c g) n")
                                dve.wait_ge(g_dve, before)
                                link(nc.vector.tensor_scalar(r, xs, 0.0, DT, ALU.max, ALU.mult))
                                for _ in range(SUB):
                                    link(nc.vector.tensor_tensor(a, v, r, ALU.add))
                                    link(nc.vector.tensor_scalar(m, a, TWO23, TWO23, ALU.min, ALU.add))
                                    link(nc.vector.tensor_scalar(n0, m, TWO23, None, ALU.subtract))
                                    link(nc.vector.tensor_tensor(f, n0, a, ALU.is_gt))
                                    link(nc.vector.tensor_tensor(n0, n0, f, ALU.subtract))
                                    link(nc.vector.tensor_tensor(v, a, n0, ALU.subtract))
                                    link(nc.vector.scalar_tensor_tensor(v, a, TWO23, v, ALU.is_lt, ALU.mult))
                                link(nc.vector.tensor_tensor(a, a, v, ALU.subtract))
                                link(nc.vector.scalar_tensor_tensor(xs, a, PER_SPIKE, xs, ALU.mult, ALU.add))
                                assert done[0] == OPS
                        dve.wait_ge(g_dve, (b + 1) * (SEQ * OPS + 1))
                        with dve.Fori(0, NC) as c:
                            with dve.Fori(0, TPC) as t:
                                dve.wait_ge(g_btp, c * TPC + t + (b * NT + 1))
                                nc.vector.tensor_copy(tile, xT[:, bass.ds(c, 1), :, bass.ds(t * P, P)]
                                                      .rearrange("p c g n -> p (c g) n")).then_inc(g_bt, 1)
                        dve.wait_ge(g_q, b + 1)
                        nc.vector.tensor_tensor(gq, ps_q, hm_b(), ALU.mult).then_inc(g_qe, 1)
                        with dve.Fori(0, NT) as t:
                            with dve.Fori(0, H) as h:
                                i = t * H + h
                                dve.wait_ge(g_mk, (t + (b * NT + 1)) * 16)
                                nc.vector.tensor_copy(onehot, sel[:, bass.ds(h * P, P)]).then_inc(g_oh, 1)
                                dve.wait_ge(g_neg, i + (b * NT * H + 1))
                                dve.wait_ge(g_bc, i + (b * NT * H + 1))
                                dve.sem_inc(g_go, 1)
                                for q in range(NC):
                                    cs = slice(q * CHUNK, (q + 1) * CHUNK)
                                    nc.vector.copy_predicated(S[:, cs], mrows[:, cs], pscore[q][:, :]).then_inc(g_cp, 1)
                                dve.wait_ge(g_cp, (i + (b * NT * H + 1)) * NC)
                                nc.vector.reduce_max(rowmax, S, AX).then_inc(g_sum, 1)
                                dve.wait_ge(g_sum, i * 2 + (b * NT * H * 2 + 1))
                                nc.vector.tensor_scalar(nrowmax, rowmax, -1.0, None, ALU.mult).then_inc(g_mx, 1)
                                dve.wait_ge(g_o, i + (b * NT * H + 1))
                                nc.vector.reciprocal(rrow, rowsum).then_inc(g_sum, 1)
                                dve.wait_ge(g_sum, i * 2 + (b * NT * H * 2 + 2))
                                nc.vector.tensor_scalar(O[:, bass.ds(h * E, E)], pin[0][:, 0:E], rrow, None,
                                                        ALU.mult).then_inc(g_O, 1)
                            dve.wait_ge(g_y, t + (b * NT + 1))
                            dve.wait_ge(g_out, (t + (b * NT + 1)) * 16)
                            nc.vector.tensor_tensor(res.unsqueeze(1), pbk[0][:, :].unsqueeze(1),
                                                    xn[:, bass.ds(t + b * NT, 1), :], ALU.add).then_inc(g_res, 1)
                dve.end_ifs()

            @block.tensor
            def _(pe):
                bad = pe.value_load(verdict[0:1, 0:1])
                with pe.If(bad > 0):
                    pe.sem_inc(g_tp, 1)
                    pe.sem_inc(g_btp, 1)
                    pe.sem_inc(g_st, 1)
                    for b in range(B):
                        with pe.Fori(0, NT) as t:
                            pe.wait_ge(g_ld, (t + (b * NT + 1)) * 16)
                            pe.wait_ge(g_ev, t + (b * NT + 1))
                            pe_transpose_tile(pin[0], [tile[:, g, :] for g in range(G)]).then_inc(g_tp, 1)
                        with pe.Fori(0, NT) as t:
                            pe.wait_ge(g_bt, t + (b * NT + 1))
                            pe.wait_ge(g_bev, t + (b * NT + 1))
                            pe_transpose_tile(pin[1], [tile[:, g, :] for g in range(G)]).then_inc(g_btp, 1)
                        pe.wait_ge(g_bev, NT * (b + 1) + 1)
                        for c in range(NC):
                            k = b * NC + c
                            pe_A_general(b, c).then_inc(g_A, 1)
                            pe.wait_ge(g_Ae, k + 1)
                            pe_Y_general(b, c).then_inc(g_Y, 1)
                        pe.wait_ge(g_ye, b + 1)
                        for j in range(G):
                            for k in range(G):
                                last = nc.tensor.matmul(ps_q[:, j, :], wqT[:, k, j * P:(j + 1) * P],
                                                        gy[:, k, j * HG:(j + 1) * HG], start=(k == 0), stop=(k == G - 1))
                        last.then_inc(g_q, 1)
                        pe.wait_ge(g_qe, b + 1)
                        for k in range(G):
                            for j in range(G):
                                last = nc.tensor.matmul(ps_w[:, k, j * HG:(j + 1) * HG],
                                                        wk_sb[:, j, k * P:(k + 1) * P], gq[:, j, :],
                                                        start=True, stop=True)
                        last.then_inc(g_w, 1)
                        pe.wait_ge(g_we, b + 1)
                        for c in range(NC):
                            if b * NC + c:
                                pe.wait_ge(g_se, b * NC + c)
                            for k in range(G):
                                last = nc.tensor.matmul(pS[0:H, :], gw[:, k, :], xT[:, c, k, :],
                                                        start=(k == 0), stop=(k == G - 1))
                            last.then_inc(g_s, 1)
                        for t in range(NT):
                            i = b * NT + t
                            if i >= 2:
                                pe.wait_ge(g_ve, i - 1)
                            for g in range(G):
                                last = nc.tensor.matmul(pbk[t % 2][:, :],
                                                        xT[:, t // TPC, g, (t % TPC) * P:(t % TPC + 1) * P],
                                                        wvT[:, g, :], start=(g == 0), stop=(g == G - 1))
                            last.then_inc(g_v, 1)
                        pe.wait_ge(g_ve, NT * (b + 1))
                        pe.wait_ge(g_se, NC * (b + 1))
                        with pe.Fori(0, NT) as t:
                            with pe.Fori(0, G) as hg:
                                with pe.Fori(0, HG) as hh:
                                    i = t * H + hg * HG + hh
                                    pe.wait_ge(g_oh, i + (b * NT * H + 1))
                                    for q in range(NC):
                                        last = nc.tensor.matmul(pscore[q][:, :], onehot,
                                                                sc[:, q * CHUNK:(q + 1) * CHUNK], start=True, stop=True)
                                    last.then_inc(g_bc, 1)
                                    pe.wait_ge(g_ex, i + (b * NT * H + 1))
                                    for q in range(NC):
                                        last = pe_transpose_tile(pturn[q], [S[:, (q * TPC + n) * P:(q * TPC + n + 1) * P]
                                                                            for n in range(TPC)])
                                    last.then_inc(g_st, 1)
                                    pe.wait_ge(g_ste, (i + (b * NT * H + 1)) * NC)
                                    for n in range(NT):
                                        vh = xT[:, n // TPC, bass.ds(hg, 1), bass.ds(hh * E + (n % TPC) * P, E)]
                                        last = nc.tensor.matmul(pin[0][:, 0:E], ST[:, n * P:(n + 1) * P],
                                                                vh.rearrange("p g n -> p (g n)"),
                                                                start=(n == 0), stop=(n == NT - 1))
                                    last.then_inc(g_o, 1)
                            pe.wait_ge(g_O, (t + (b * NT + 1)) * H)
                            pe_transpose_tile(pin[1], [O[:, j * P:(j + 1) * P] for j in range(G)]).then_inc(g_ot, 1)
                            pe.wait_ge(g_ote, t + (b * NT + 1))
                            for j in range(G):
                                last = nc.tensor.matmul(pbk[0][:, :], OT[:, j, :], woT[:, j, :], start=(j == 0),
                                                        stop=(j == G - 1))
                            last.then_inc(g_y, 1)
                pe.end_ifs()


_INS = ['x', 'cond_1024', 'mask_SxS_bk0', 'L1_cond_Wq', 'L1_cond_Wk', 'L1_cond_Wv', 'L1_cond_Wt', 'L1_cond_Wo']
_OUTS = [((2, 2048, 512), 'float32')]


def kernel(**inputs):
    import numpy as _np
    import concourse.bacc as _bacc
    from concourse import mybir as _mybir
    from concourse.bass_utils import run_bass_kernel_spmd as _run

    nc = _bacc.Bacc("TRN2", target_bir_lowering=False, num_devices=1)
    arrays, args = {}, []
    for name in _INS:
        a = _np.ascontiguousarray(inputs[name])
        arrays[f"in_{name}_dram"] = a
        args.append(nc.dram_tensor(f"in_{name}_dram", a.shape, _mybir.dt.from_np(a.dtype), kind="ExternalInput").ap())
    for i, (shape, dtype) in enumerate(_OUTS):
        dt = _mybir.dt.from_np(_np.dtype(dtype))
        args.append(nc.dram_tensor(f"out_{i}_dram", shape, dt, kind="ExternalOutput").ap())
    spiking_residual_attention(nc, *args)
    r = _run(nc, [arrays], core_ids=[0])
    got = tuple(r.results[0][f"out_{i}_dram"] for i in range(len(_OUTS)))
    return got[0]
```
